# Optimizing a Trainium2 kernel written in Bass

```python
import numpy as np
import jax
import jax.numpy as jnp

def _softmax(x, axis=-1):
    return jax.nn.softmax(x, axis=axis)

def _gelu(x):
    return jax.nn.gelu(x, approximate=True)

def _silu(x):
    return jax.nn.silu(x)

def _sigmoid(x):
    return jax.nn.sigmoid(x)

def _layernorm(x, axis=-1, eps=1e-05):
    m = jnp.mean(x, axis=axis, keepdims=True)
    v = jnp.var(x, axis=axis, keepdims=True)
    return (x - m) / jnp.sqrt(v + eps)

def _scatter_add(tgt, idx, src, axis=0):
    return tgt.at[idx].add(src)

def _segment_sum(src, seg, n):
    return jax.ops.segment_sum(src, seg, n)
kernel_name = 'mk_gnn_preln_d2_gnn_r8_08af9c'

def setup_inputs(seed: int=0):
    np.random.seed(seed)
    _w = jnp.asarray

    def _rec_inputs():
        import jax
        import jax.numpy as jnp
        _gk = jax.random.key(seed)
        x = -0.000202 + 1 * jax.random.normal(jax.random.fold_in(_gk, 1), (12500, 64), jnp.float32)
        _s = jax.random.randint(jax.random.fold_in(_gk, 2), (200000,), 0, 12500, jnp.int32)
        _d = jax.random.randint(jax.random.fold_in(_gk, 3), (200000,), 0, 12500, jnp.int32)
        _loop = jnp.arange(12500, dtype=jnp.int32)
        src = jnp.concatenate([_s, _d, _loop])
        dst = jnp.concatenate([_d, _s, _loop])
        _o = jnp.argsort(dst, stable=True)
        src = src[_o]
        dst = dst[_o]
        return (x, src, dst)
    x, src, dst = _rec_inputs()

    def _L0_gnn_setup():
        import jax, jax.numpy as jnp
        import numpy as np
        N_SRC = 12500
        N_EDGES = 125000
        IN_FEATS = 64
        N_CLASSES = 64
        key = jax.random.key(seed)
        k1, k2, k3, k4, k5 = jax.random.split(key, 5)
        x = jax.random.normal(k1, (N_SRC, IN_FEATS), dtype=jnp.float32)
        W_self = jax.random.normal(k2, (IN_FEATS, N_CLASSES), dtype=jnp.float32) / np.sqrt(IN_FEATS)
        W_neigh = jax.random.normal(k3, (IN_FEATS, N_CLASSES), dtype=jnp.float32) / np.sqrt(IN_FEATS)
        b = jnp.zeros((N_CLASSES,), dtype=jnp.float32)
        src = jax.random.randint(k4, (N_EDGES,), 0, N_SRC, dtype=jnp.int32)
        dst = jax.random.randint(k5, (N_EDGES,), 0, N_SRC, dtype=jnp.int32)
        return {'x': x, 'W_self': W_self, 'W_neigh': W_neigh, 'b': b, 'src': src, 'dst': dst, 'num_dst': N_SRC}
    _L0_gnn_all = _L0_gnn_setup()
    _L0_gnn_in = {k: v for k, v in _L0_gnn_all.items() if k in ('W_self', 'W_neigh', 'b')}
    del _L0_gnn_all

    def _L1_gnn_setup():
        import jax, jax.numpy as jnp
        import numpy as np
        N_NODES = 12500
        N_EDGES = 125000
        D = 64
        H = 128
        key = jax.random.key(seed)
        ks = jax.random.split(key, 12)
        x = jax.random.normal(ks[0], (N_NODES, D), dtype=jnp.float32)
        start = jax.random.randint(ks[1], (N_EDGES,), 0, N_NODES)
        end = jax.random.randint(ks[2], (N_EDGES,), 0, N_NODES)

        def w(k, fan_in, shape):
            return jax.random.normal(k, shape, dtype=jnp.float32) / jnp.sqrt(jnp.float32(fan_in))
        We1 = w(ks[3], 2 * D, (2 * D, H))
        be1 = jnp.zeros((H,), jnp.float32)
        We2 = w(ks[4], H, (H, 1))
        be2 = jnp.zeros((1,), jnp.float32)
        Wn1 = w(ks[5], 3 * D, (3 * D, H))
        bn1 = jnp.zeros((H,), jnp.float32)
        Wn2 = w(ks[6], H, (H, D))
        bn2 = jnp.zeros((D,), jnp.float32)
        return {'x': x, 'start': start, 'end': end, 'We1': We1, 'be1': be1, 'We2': We2, 'be2': be2, 'Wn1': Wn1, 'bn1': bn1, 'Wn2': Wn2, 'bn2': bn2}
    _L1_gnn_all = _L1_gnn_setup()
    _L1_gnn_in = {k: v for k, v in _L1_gnn_all.items() if k in ('We1', 'be1', 'We2', 'be2', 'Wn1', 'bn1', 'Wn2', 'bn2')}
    del _L1_gnn_all
    return {'x': x, 'src': src, 'dst': dst, 'L0_gnn_W_self': _L0_gnn_in['W_self'], 'L0_gnn_W_neigh': _L0_gnn_in['W_neigh'], 'L0_gnn_b': _L0_gnn_in['b'], 'L1_gnn_We1': _L1_gnn_in['We1'], 'L1_gnn_be1': _L1_gnn_in['be1'], 'L1_gnn_We2': _L1_gnn_in['We2'], 'L1_gnn_be2': _L1_gnn_in['be2'], 'L1_gnn_Wn1': _L1_gnn_in['Wn1'], 'L1_gnn_bn1': _L1_gnn_in['bn1'], 'L1_gnn_Wn2': _L1_gnn_in['Wn2'], 'L1_gnn_bn2': _L1_gnn_in['bn2']}

def reference(x, src, dst, L0_gnn_W_self, L0_gnn_W_neigh, L0_gnn_b, L1_gnn_We1, L1_gnn_be1, L1_gnn_We2, L1_gnn_be2, L1_gnn_Wn1, L1_gnn_bn1, L1_gnn_Wn2, L1_gnn_bn2):
    import jax
    import jax.numpy as jnp

    def _L0_gnn_ref(x, W_self, W_neigh, b, src, dst, num_dst):
        import jax, jax.numpy as jnp
        import numpy as np
        N_SRC = 12500
        N_EDGES = 125000
        IN_FEATS = 64
        N_CLASSES = 64
        msgs = x[src]
        summed = jax.ops.segment_sum(msgs, dst, num_segments=num_dst)
        deg = jax.ops.segment_sum(jnp.ones((src.shape[0],), x.dtype), dst, num_segments=num_dst)
        h_neigh = summed / jnp.maximum(deg, 1.0)[:, None]
        h_dst = x[:num_dst]
        h = h_dst @ W_self + h_neigh @ W_neigh + b
        return jax.nn.relu(h)

    def _L1_gnn_ref(x, start, end, We1, be1, We2, be2, Wn1, bn1, Wn2, bn2):
        import jax, jax.numpy as jnp
        import numpy as np
        N_NODES = 12500
        N_EDGES = 125000
        D = 64
        H = 128
        n = x.shape[0]
        xs = x[start]
        edge_inputs = jnp.concatenate([xs, x[end]], axis=1)
        h = jax.nn.relu(edge_inputs @ We1 + be1)
        e = jax.nn.sigmoid(h @ We2 + be2)
        m = e * xs
        m_sum = jax.ops.segment_sum(m, end, num_segments=n)
        m_max = jax.ops.segment_max(m, end, num_segments=n)
        m_max = jnp.where(jnp.isneginf(m_max), jnp.float32(0.0), m_max)
        messages = jnp.concatenate([m_max, m_sum], axis=-1)
        node_inputs = jnp.concatenate([messages, x], axis=1)
        h2 = jax.nn.relu(node_inputs @ Wn1 + bn1)
        x_out = h2 @ Wn2 + bn2 + x
        return x_out
    h = jnp.maximum(_layernorm(x, axis=-1), 0.0)
    x = x + _L0_gnn_ref(h, L0_gnn_W_self, L0_gnn_W_neigh, L0_gnn_b, src, dst, 12500)
    h = jnp.maximum(_layernorm(x, axis=-1), 0.0)
    x = x + _L1_gnn_ref(h, src, dst, L1_gnn_We1, L1_gnn_be1, L1_gnn_We2, L1_gnn_be2, L1_gnn_Wn1, L1_gnn_bn1, L1_gnn_Wn2, L1_gnn_bn2)
    return x

_drawn_inputs = setup_inputs


def setup_inputs(seed=0):
    import zlib

    import numpy as np

    out = dict(_drawn_inputs(seed))
    spreads = {'L0_gnn_b': (0.0, 0.1),
     'L1_gnn_be1': (0.0, 0.1),
     'L1_gnn_bn1': (0.0, 0.415),
     'L1_gnn_bn2': (0.0, 0.1)}
    factors = {}
    for name, (base, spread) in spreads.items():
        noise = np.random.default_rng([zlib.crc32(name.encode()), seed]).standard_normal(out[name].shape)
        drawn = base * np.exp(spread * noise) if base else spread * noise
        out[name] = jnp.asarray(drawn.astype(out[name].dtype))
    for name, factor in factors.items():
        out[name] = (out[name] * factor).astype(out[name].dtype)
    return out
```

```python
from contextlib import ExitStack

import concourse.bass as bass
from concourse import mybir

F32 = mybir.dt.float32
BF16 = mybir.dt.bfloat16
I32 = mybir.dt.int32
ALU = mybir.AluOpType
ACT = mybir.ActivationFunctionType
AX = mybir.AxisListType

P = 128
EPS = 1e-5

SLOTS = 4
STAGES = 2
STAGE_COLS = 16
GROUP_COLS = STAGES * STAGE_COLS
RING = GROUP_COLS // SLOTS
STAGE_CHUNKS = STAGE_COLS // SLOTS

RUN = 64
BINS = 64
SEARCH_ROW2 = 64
SEARCH_ROW3 = 128


class Steps:

    def __init__(self, eng, sem, alone):
        self.eng, self.sem, self.alone, self.base, self.n = eng, sem, alone, 0, 0

    def done(self, ins):
        ins.then_inc(self.sem, 1)
        self.n += 1

    def wait(self):
        self.eng.wait_ge(self.sem, self.base + self.n)

    def link(self, ins):
        self.done(ins)
        self.wait()

    def link_alone(self, ins):
        self.done(ins)
        self.alone(self.eng, self.sem, self.base + self.n)

    def at(self, base):
        self.base, self.n = base, 0

    def now(self):
        return self.base + self.n


def gnn_kernel(nc, x, src, dst, w_self, w_neigh, b0, we1, be1, we2, be2, wn1, bn1, wn2, bn2, out):
    N, D = x.shape
    E = src.shape[0]
    H = we1.shape[1]
    T = -(-N // P)
    NP = T * P
    ZROW = NP
    NROWS = NP + 1
    FULL = N // T
    REST = N - FULL * T

    ROWS3 = -(-E // SEARCH_ROW3)
    TOP = -(-ROWS3 // SEARCH_ROW2)
    ROWS3P = TOP * SEARCH_ROW2
    DPAD = ROWS3P * SEARCH_ROW3
    DTAIL = DPAD - E
    TAILP = next(p for p in range(P, 0, -1) if DTAIL % p == 0)

    SHALF = 10
    SITER = -(-(T + 1) // (2 * SHALF))
    SCOLS = SITER * 2 * SHALF
    THALF = 7
    TITER = T // (2 * THALF)
    assert TITER * 2 * THALF == T and T <= P

    SRC_ROWS = -(-(E + RUN) // RUN)
    SRC_PAD = SRC_ROWS * RUN - E
    MAXCOLS = E + 2 * T * SLOTS
    MAXCHUNKS = MAXCOLS // SLOTS
    MAXBLOCKS = E // RUN + T + 1
    STREAM = (MAXCOLS // RUN + 3) * RUN

    def dram(name, shape, dt):
        return nc.dram_tensor(name, shape, dt).ap()

    dst_rows = dram("dst_rows", (ROWS3P, SEARCH_ROW3), I32)
    dst_row_starts = dram("dst_row_starts", (TOP, SEARCH_ROW2), I32)
    src_pad = dram("src_pad", (SRC_ROWS, RUN), I32)
    x_pad = dram("x_pad", (NP, D), F32)
    h0_table = dram("h0_table", (NROWS, D), F32)
    records = dram("records", (NP, 4), I32)
    stream = dram("stream", (P, STREAM), I32)
    WROW = D + H
    ranked_rows = dram("ranked_rows", (P, T * (WROW + 1)), F32)
    hA_table = dram("hA_table", (NROWS, WROW), F32)

    with ExitStack() as ctx:
        def sb(name, shape, dt=F32):
            return ctx.enter_context(nc.sbuf_tensor(name, shape, dt))

        def psum(name, shape):
            return ctx.enter_context(nc.psum_tensor(name, shape, F32))

        def sem(name):
            return ctx.enter_context(nc.semaphore(name))

        ident = sb("ident", [P, P])
        upper = sb("upper", [P, P])
        ones = sb("ones", [P, P])
        w_cat = sb("w_cat", [2 * D, D])
        w_ab = sb("w_ab", [D, 2 * H])
        w_n1a = sb("w_n1a", [2 * D, H])
        w_n1b = sb("w_n1b", [D, H])
        w_n2 = sb("w_n2", [H, D])
        b0_row = sb("b0_row", [1, D])
        be1_row = sb("be1_row", [1, H])
        bn2_row = sb("bn2_row", [1, D])
        bn1_col = sb("bn1_col", [H, 1])
        be2_col = sb("be2_col", [P, 1])
        eps_col = sb("eps_col", [P, 1])
        we2_rows = sb("we2_rows", [P, H])
        big_tail = sb("big_tail", [P, max(DTAIL // TAILP, SRC_PAD)], I32)
        zeros = sb("zeros", [P, WROW])
        zcols = sb("zcols", [P, RUN], I32)

        rec = sb("rec", [P, T, 5], I32)
        ranked = sb("ranked", [P, T, 4], I32)
        deg = sb("deg", [P, T])
        rdeg = sb("rdeg", [P, T])
        ctl = sb("ctl", [1, T, 4], I32)
        tot = sb("tot", [1, 4], I32)
        xr = sb("xr", [P, T, D])
        hr = sb("hr", [P, T, D])
        b_self = sb("b_self", [P, T, H])
        ring = sb("ring", [P, GROUP_COLS * WROW])
        stage = sb("stage", [P, STAGES, STAGE_COLS], I32)

        x_nodes = b_self[:, :, 0:D]
        h_nodes = b_self[:, :, D:2 * D]
        onehot = hr

        q = sb("q", [P, SCOLS])
        top = sb("top", [P, TOP])
        top_i = sb("top_i", [P, TOP], I32)
        row2 = sb("row2", [P, SCOLS])
        row3 = sb("row3", [P, SCOLS])
        start = sb("start", [P, SCOLS])
        cnt = sb("cnt", [P, SHALF])
        sstage = sb("sstage", [P, 2, SHALF], I32)
        got2 = sb("got2", [P, 2, SHALF, SEARCH_ROW2], I32)
        got3 = sb("got3", [P, 2, SHALF, SEARCH_ROW3], I32)
        cmp3 = sb("cmp3", [P, SHALF, SEARCH_ROW3])
        cols = sb("cols", [P, T])
        cols2 = sb("cols2", [P, T])
        cols3 = sb("cols3", [P, T])
        icols = sb("icols", [P, T], I32)
        icols2 = sb("icols2", [P, T], I32)
        bins = sb("bins", [P, T])
        bin_b = sb("bin_b", [P, T], BF16)
        iota_bin = sb("iota_bin", [P, BINS])
        iota_run = sb("iota_run", [P, RUN])
        iota_i = sb("iota_i", [P, RUN], I32)
        q_i = sb("q_i", [P, SCOLS], I32)
        bin_tot = sb("bin_tot", [P, BINS])
        bin_scan = sb("bin_scan", [P, BINS])
        bin_off = sb("bin_off", [P, BINS])
        rank_rec = sb("rank_rec", [P, 2, THALF, 5], I32)
        tstage = sb("tstage", [P, 2, THALF, 2], I32)
        xland = sb("xland", [P, 2, THALF, D])
        runs = sb("runs", [P, 2, THALF, RUN], I32)
        runs_m = sb("runs_m", [P, 2, THALF, RUN], I32)
        valid = sb("valid", [P, THALF, RUN])
        crow = sb("crow", [1, 4, T])
        irow = sb("irow", [1, 4, T], I32)
        one1 = sb("one1", [1, T])

        cat = sb("cat", [P, 2 * D])
        catT = sb("catT", [P, P])
        hT = sb("hT", [D, P])
        h_tile = sb("h_tile", [P, D])
        h2T = sb("h2T", [H, P])
        rowbuf = sb("rowbuf", [P, WROW + 1])
        stats = sb("stats", [P, 6])
        mv = sb("mv", [P, 2])
        std = sb("std", [P, 1])
        rstd = sb("rstd", [P, 1])
        pre = sb("pre", [P, SLOTS, H])
        act_w = sb("act_w", [P, SLOTS, H])
        z = sb("z", [P, SLOTS])
        gate = sb("gate", [P, SLOTS])
        msg = sb("msg", [P, SLOTS, D])
        chunk_max = sb("chunk_max", [P, D])

        pairs = ring[:, 0:T * T // 2 + 1].bitcast(BF16)[:, 0:T * T].rearrange("p (a b) -> p a b", a=T)
        cmp1 = ring[:, 0:SCOLS * TOP].rearrange("p (a b) -> p a b", a=SCOLS)
        fin_rows = ring[:, 0:2 * THALF * (WROW + 1)].rearrange("p (h t w) -> p h t w", h=2, t=THALF)
        ring0 = ring[:, 0:GROUP_COLS * D].rearrange("p (c s w) -> p c s w", c=RING, s=SLOTS)
        ring1 = ring[:, :].rearrange("p (c s w) -> p c s w", c=RING, s=SLOTS)
        out_rows = xland
        out_idx = tstage

        ps_sum = psum("ps_sum", [P, 512])
        ps_t = psum("ps_t", [P, 512])
        ps_u = psum("ps_u", [P, 512])
        ps_y = psum("ps_y", [P, 512])
        ps_a = psum("ps_a", [P, 512])
        ps_h = psum("ps_h", [P, 512])

        s_passed = sem("s_passed")
        s_const = sem("s_const")
        s_zero = sem("s_zero")
        s_top = sem("s_top")
        s_w = sem("s_w")
        s_x = sem("s_x")
        s_tab = sem("s_tab")
        s_dve = sem("s_dve")
        s_idx2 = sem("s_idx2")
        s_got2 = [sem(f"s_got2{h}") for h in range(2)]
        s_idx3 = sem("s_idx3")
        s_got3 = [sem(f"s_got3{h}") for h in range(2)]
        s_bins = sem("s_bins")
        s_binp = sem("s_binp")
        s_pair = sem("s_pair")
        s_gen = sem("s_gen")
        s_rfree = sem("s_rfree")
        s_rec = sem("s_rec")
        s_recw = [sem(f"s_recw{h}") for h in range(2)]
        s_rank = sem("s_rank")
        s_var = sem("s_var")
        s_std = sem("s_std")
        s_h0 = sem("s_h0")
        s_h0w = sem("s_h0w")
        s_degf = sem("s_degf")
        s_degT = sem("s_degT")
        s_mxc = sem("s_mxc")
        s_mxr = sem("s_mxr")
        s_ctl = sem("s_ctl")
        s_tidx = sem("s_tidx")
        s_land = [sem(f"s_land{h}") for h in range(2)]
        s_mask = sem("s_mask")
        s_wr = sem("s_wr")
        s_blk = sem("s_blk")
        s_blkl = sem("s_blkl")
        s_blkm = sem("s_blkm")
        s_blkw = sem("s_blkw")
        s_free = sem("s_free")
        s_stream = sem("s_stream")
        s_hr = sem("s_hr")

        class Layer:
            def __init__(self, n):
                self.staged = [sem(f"s_staged{n}_{h}") for h in range(STAGES)]
                self.got = [sem(f"s_got{n}_{c}") for c in range(RING)]
                self.landed = sem(f"s_landed{n}")
                self.used = sem(f"s_used{n}")
                self.sum = sem(f"s_sum{n}")
                self.cat = sem(f"s_cat{n}")
                self.catT = sem(f"s_catT{n}")
                self.catTs = sem(f"s_catTs{n}")
                self.y = sem(f"s_y{n}")
                self.tile = sem(f"s_tile{n}")

        l0, l1 = Layer(0), Layer(1)
        s_var1 = sem("s_var1")
        s_std1 = sem("s_std1")
        s_h1 = sem("s_h1")
        s_h1T = sem("s_h1T")
        s_h1Ts = sem("s_h1Ts")
        s_ab = sem("s_ab")
        s_rowA = sem("s_rowA")
        s_row = sem("s_row")
        s_fin = [sem(f"s_fin{h}") for h in range(2)]
        s_finw = [sem(f"s_finw{h}") for h in range(2)]
        s_pre = sem("s_pre")
        s_act = sem("s_act")
        s_acc = sem("s_acc")
        s_z = sem("s_z")
        s_gate = sem("s_gate")
        s_msg = sem("s_msg")
        s_msgf = sem("s_msgf")
        s_hid = sem("s_hid")
        s_hids = sem("s_hids")
        s_outs = sem("s_outs")
        s_outw = [sem(f"s_outw{h}") for h in range(2)]

        def tile_counts(eng, i):
            n = eng.value_load(ctl[0:1, bass.ds(i, 1), 0:1].rearrange("p a b -> p (a b)"), min_val=2, max_val=MAXCHUNKS)
            before = eng.value_load(ctl[0:1, bass.ds(i, 1), 1:2].rearrange("p a b -> p (a b)"), min_val=0, max_val=MAXCHUNKS)
            return n, before

        def groups(eng):
            return eng.value_load(tot[0:1, 1:2], min_val=1, max_val=MAXCHUNKS // RING + 1)

        def total_chunks(eng):
            return eng.value_load(tot[0:1, 0:1], min_val=T, max_val=MAXCHUNKS)

        def extra_blocks(eng):
            return eng.value_load(tot[0:1, 2:3], min_val=0, max_val=MAXBLOCKS)

        def tile_blocks(eng, i):
            n = eng.value_load(ctl[0:1, bass.ds(i, 1), 2:3].rearrange("p a b -> p (a b)"), min_val=1, max_val=MAXBLOCKS)
            before = eng.value_load(ctl[0:1, bass.ds(i, 1), 3:4].rearrange("p a b -> p (a b)"), min_val=0, max_val=MAXBLOCKS)
            return n, before

        def at_tile(t, i, lo=0, hi=None):
            hi = t.shape[2] if hi is None else hi
            return t[:, bass.ds(i, 1), lo:hi].rearrange("p a b -> p (a b)")

        def wait_alone(eng, s, value):
            eng.wait_ge(s, value)
            eng.sem_inc(s_passed, 1)

        TAB_DMAS = 16 * 8
        X_DMAS = 16 * (2 if REST else 1)
        W_DMAS = 16 * 13

        block = ctx.enter_context(nc.Block())

        @block.gpsimd
        def _(pool):
            pool.iota(q_i[:, :], pattern=[[1, SCOLS]], base=0, channel_multiplier=T).then_inc(s_const, 1)
            pool.iota(iota_i[:, :], pattern=[[1, RUN]], base=0, channel_multiplier=0).then_inc(s_const, 1)
            pool.wait_ge(s_zero, 1)
            pool.affine_select(out=ident[:, :], in_=ones[:, :], compare_op=ALU.is_equal, fill=0.0, base=0,
                               pattern=[[-1, P]], channel_multiplier=1).then_inc(s_const, 1)
            pool.affine_select(out=upper[:, :], in_=ones[:, :], compare_op=ALU.is_gt, fill=0.0, base=0,
                               pattern=[[1, P]], channel_multiplier=-1).then_inc(s_const, 1)

            def gather(to, table, idx, axis=0):
                return pool.indirect_dma_start(to, None, table, bass.IndirectOffsetOnAxis(ap=idx, axis=axis))

            pool.wait_ge(s_tab, TAB_DMAS)
            for idx_ready, got_sem, got, table in ((s_idx2, s_got2, got2, dst_row_starts),
                                                   (s_idx3, s_got3, got3, dst_rows)):
                with pool.Fori(0, SITER) as it:
                    for h in range(2):
                        wait_alone(pool, idx_ready, 2 * it + h + 1)
                        for k in range(SHALF):
                            gather(got[:, h, k, :], table[:, :], sstage[:, h, k:k + 1]).then_inc(got_sem[h], 16)

            pool.wait_ge(s_pair, 1)
            pool.affine_select(out=pairs, in_=pairs, compare_op=ALU.is_gt, fill=0.0, base=0,
                               pattern=[[1, T], [-1, T]], channel_multiplier=0).then_inc(s_const, 1)

            with pool.Fori(0, TITER) as it:
                for h in range(2):
                    wait_alone(pool, s_rec, 2 * it + h + 1)
                    for k in range(THALF):
                        pool.indirect_dma_start(
                            records[:, :], bass.IndirectOffsetOnAxis(ap=rank_rec[:, h, k, 4:5], axis=0),
                            rank_rec[:, h, k, 0:4], None).then_inc(s_recw[h], 16)

            pool.wait_ge(s_ctl, 2)
            extra = extra_blocks(pool)
            with pool.If(extra > 0):
                with pool.Fori(0, T) as i:
                    n, before = tile_blocks(pool, i)
                    with pool.Fori(0, n) as b:
                        wait_alone(pool, s_blk, before + b + 1)
                        gather(runs[:, 0, 0, :], src_pad[:, :], tstage[:, 0, 0, 1:2], axis=1).then_inc(s_blkl, 16)

            with pool.Fori(0, TITER) as it:
                for h in range(2):
                    wait_alone(pool, s_tidx, 2 * it + h + 1)
                    for k in range(THALF):
                        gather(runs[:, h, k, :], src_pad[:, :], tstage[:, h, k, 1:2], axis=1).then_inc(s_land[h], 16)
                    for k in range(THALF):
                        gather(xland[:, h, k, :], x_pad[:, :], tstage[:, h, k, 0:1]).then_inc(s_land[h], 16)

            def gather_layer(ly, table, places, ready, ready_at):
                pool.wait_ge(ready, ready_at)
                with pool.Fori(0, groups(pool)) as g:
                    for h in range(STAGES):
                        wait_alone(pool, ly.staged[h], 16 * (g + 1))
                        for c in range(STAGE_CHUNKS * h, STAGE_CHUNKS * (h + 1)):
                            wait_alone(pool, ly.used, RING * g + c + 1)
                            for s in range(SLOTS):
                                col = (c * SLOTS + s) % STAGE_COLS
                                gather(places[:, c, s, :], table[:, :],
                                       stage[:, h, col:col + 1]).then_inc(ly.got[c], 16)

            gather_layer(l0, h0_table, ring0, s_h0w, 32)

            with pool.Fori(0, TITER) as it:
                for h in range(2):
                    wait_alone(pool, s_fin[h], 16 * (it + 1))
                    for k in range(THALF):
                        pool.indirect_dma_start(
                            hA_table[:, :],
                            bass.IndirectOffsetOnAxis(ap=fin_rows[:, h, k, WROW:WROW + 1].bitcast(I32), axis=0),
                            fin_rows[:, h, k, 0:WROW], None).then_inc(s_finw[h], 16)
            for h in range(2):
                pool.wait_ge(s_finw[h], 16 * THALF * TITER)
            gather_layer(l1, hA_table, ring1, s_row, 16)

            with pool.Fori(0, TITER) as it:
                for h in range(2):
                    wait_alone(pool, s_outs, 4 * it + 2 * h + 2)
                    for k in range(THALF):
                        pool.indirect_dma_start(
                            out[:, :], bass.IndirectOffsetOnAxis(ap=out_idx[:, h, k, 0:1], axis=0),
                            out_rows[:, h, k, :], None, bounds_check=N - 1,
                            oob_is_err=False).then_inc(s_outw[h], 16)
            for h in range(2):
                pool.wait_ge(s_outw[h], 16 * THALF * TITER)

        @block.sync
        def _(sp):
            flat_rows = dst_rows.rearrange("a b -> (a b)")
            flat_starts = dst_row_starts.rearrange("a b -> (a b)")
            with nc.allow_non_contiguous_dma(reason="every 128th entry of the sorted list"):
                step1 = SEARCH_ROW2 * SEARCH_ROW3
                nfull = E // step1
                sp.dma_start(top_i[:, 0:nfull],
                             dst[0:nfull * step1].rearrange("(a b) -> a b", b=step1)[:, 0:1].rearrange(
                                 "a b -> b a").partition_broadcast(P).rearrange("p b a -> p (b a)")
                             ).then_inc(s_top, 16)
                sp.dma_start(top_i[:, nfull:TOP],
                             dst[nfull * step1:nfull * step1 + 1].unsqueeze(0).to_broadcast([P, 1])
                             ).then_inc(s_top, 16)
                sp.dma_start(flat_starts[0:ROWS3 - 1],
                             dst[0:(ROWS3 - 1) * SEARCH_ROW3].rearrange("(a b) -> a b", b=SEARCH_ROW3)[:, 0:1]
                             .rearrange("a b -> (a b)")).then_inc(s_tab, 16)
            sp.dma_start(flat_starts[ROWS3 - 1:ROWS3],
                         dst[(ROWS3 - 1) * SEARCH_ROW3:(ROWS3 - 1) * SEARCH_ROW3 + 1]).then_inc(s_tab, 16)
            sp.dma_start(flat_rows[0:E], dst[:]).then_inc(s_tab, 16)
            sp.wait_ge(s_zero, 2)
            sp.dma_start(flat_rows[E:DPAD].rearrange("(a b) -> a b", a=TAILP),
                         big_tail[0:TAILP, 0:DTAIL // TAILP]).then_inc(s_tab, 16)
            sp.dma_start(flat_starts[ROWS3:ROWS3P].unsqueeze(0), big_tail[0:1, 0:ROWS3P - ROWS3]).then_inc(s_tab, 16)
            sp.dma_start(x_nodes[0:FULL], x[0:FULL * T, :].rearrange("(p t) d -> p t d", p=FULL)).then_inc(s_x, 16)
            if REST:
                sp.dma_start(x_nodes[FULL:FULL + 1, 0:REST], x[FULL * T:N, :].unsqueeze(0)).then_inc(s_x, 16)
            flat_src = src_pad.rearrange("a b -> (a b)")
            sp.dma_start(flat_src[0:E], src[:]).then_inc(s_tab, 16)
            sp.dma_start(flat_src[E:E + SRC_PAD].unsqueeze(0), big_tail[0:1, 0:SRC_PAD]).then_inc(s_tab, 16)
            sp.wait_ge(s_x, X_DMAS)
            sp.dma_start(x_pad.rearrange("(p t) d -> p t d", p=P), x_nodes).then_inc(s_tab, 16)

            for h in range(2):
                sp.wait_ge(s_recw[h], 16 * THALF * TITER)
            sp.dma_start(ranked[:, :, :], records.rearrange("(p t) w -> p t w", p=P)).then_inc(s_rank, 16)

            sp.wait_ge(s_ctl, 2)
            extra = extra_blocks(sp)
            with sp.If(extra > 0):
                with sp.Fori(0, T) as i:
                    n, before = tile_blocks(sp, i)
                    _, chunks_before = tile_counts(sp, i)
                    with sp.Fori(0, n) as b:
                        sp.wait_ge(s_blkm, before + b + 1)
                        col = nc.s_assert_within(chunks_before * SLOTS + b * RUN, 0, STREAM - RUN,
                                                 skip_runtime_bounds_check_because="a tile's blocks start before its end")
                        sp.dma_start(stream[:, bass.ds(col, RUN)], runs_m[:, 0, 0, :]).then_inc(s_blkw, 16)
            sp.sem_inc(s_rfree, 2)
            with sp.Fori(0, TITER) as it:
                for h in range(2):
                    sp.wait_ge(s_mask, 2 * it + h + 1)
                    for k in range(THALF):
                        i = (2 * it + h) * THALF + k
                        _, before = tile_counts(sp, i)
                        sp.dma_start(stream[:, bass.ds(before * SLOTS, RUN)], runs_m[:, h, k, :]).then_inc(s_wr, 16)
                        sp.wait_ge(s_wr, (2 * it + h) * (16 * THALF) + 16 * (k + 1))
                    sp.sem_inc(s_rfree, 1)
            chunks = total_chunks(sp)
            sp.dma_start(stream[:, bass.ds(chunks * SLOTS, RUN)], zcols[:, :]).then_inc(s_wr, 16)
            sp.wait_ge(s_wr, 16 * (T + 1))

            def relay_layer(ly):
                for h in range(STAGES):
                    sp.dma_start(stage[:, h, :], stream[:, h * STAGE_COLS:(h + 1) * STAGE_COLS]
                                 ).then_inc(ly.staged[h], 16)
                n = groups(sp)
                with sp.Fori(0, n) as g:
                    for h in range(STAGES):
                        for c in range(STAGE_CHUNKS * h, STAGE_CHUNKS * (h + 1)):
                            sp.wait_ge(ly.got[c], 16 * SLOTS * (g + 1))
                            sp.sem_inc(ly.landed, 1)
                        sp.dma_start(stage[:, h, :], stream[:, bass.ds(g * GROUP_COLS + GROUP_COLS + h * STAGE_COLS, STAGE_COLS)]
                                     ).then_inc(ly.staged[h], 16)
                for h in range(STAGES):
                    wait_alone(sp, ly.staged[h], 16 * (n + 1))

            relay_layer(l0)

            sp.wait_ge(s_row, 16 * (T + 1))
            half = THALF * (WROW + 1)
            for h in range(2):
                sp.dma_start(fin_rows[:, h, :, :].rearrange("p t w -> p (t w)"),
                             ranked_rows[:, h * half:(h + 1) * half]).then_inc(s_fin[h], 16)
            with sp.Fori(0, TITER - 1) as it:
                for h in range(2):
                    sp.wait_ge(s_finw[h], 16 * THALF * (it + 1))
                    sp.dma_start(fin_rows[:, h, :, :].rearrange("p t w -> p (t w)"),
                                 ranked_rows[:, bass.ds(it * (2 * half) + (2 + h) * half, half)]).then_inc(s_fin[h], 16)
            relay_layer(l1)

        @block.vector
        def _(v):
            st = Steps(v, s_dve, wait_alone)

            def bc(t, n):
                return t.unsqueeze(2).to_broadcast([t.shape[0], t.shape[1], n])

            def bc_mid(t, n):
                return t.unsqueeze(1).to_broadcast([t.shape[0], n, t.shape[1]])

            v.memset(ones[:, :], 1.0).then_inc(s_zero, 1)
            st.done(v.memset(zeros[:, :], 0.0))
            st.done(v.memset(one1[:, :], 1.0))
            st.done(v.memset(big_tail[:, :], NP))
            st.done(v.memset(zcols[:, :], ZROW))
            st.done(v.memset(eps_col[:, :], EPS))
            st.done(v.memset(rec[:, :, :], 0))
            st.link(v.memset(x_nodes[96:P], 0.0))
            v.memset(stats[:, :], 0.0).then_inc(s_zero, 1)

            v.wait_ge(s_const, 4)
            st.done(v.tensor_copy(q[:, :], q_i[:, :]))
            st.done(v.tensor_copy(iota_bin[:, :], iota_i[:, 0:BINS]))
            st.done(v.tensor_copy(iota_run[:, :], iota_i[:, :]))
            v.wait_ge(s_top, 32)
            st.link(v.tensor_copy(top[:, :], top_i[:, :]))
            st.link(v.tensor_tensor(cmp1, bc_mid(top[:, :], SCOLS), bc(q[:, :], TOP), ALU.is_lt))
            st.link(v.tensor_reduce(row2[:, :], cmp1, AX.X, ALU.add))
            st.link(v.tensor_scalar(row2[:, :], row2[:, :], -1.0, 0.0, ALU.add, ALU.max))

            def search(rows, idx_sem, got_sem, got, width, result):
                middle = result is row3

                def stage_rows(cols_at, h):
                    v.tensor_copy(sstage[:, h, :], rows[:, cols_at]).then_inc(idx_sem, 1)

                def count(cols_at, h):
                    st.link(v.tensor_tensor(cmp3[:, :, 0:width], got[:, h, :, :], bc(q[:, cols_at], width), ALU.is_lt))
                    st.link(v.tensor_reduce(cnt[:, :], cmp3[:, :, 0:width], AX.X, ALU.add))
                    if middle:
                        st.link(v.tensor_scalar(cnt[:, :], cnt[:, :], -1.0, 0.0, ALU.add, ALU.max))
                    st.link_alone(v.scalar_tensor_tensor(out=result[:, cols_at], in0=rows[:, cols_at],
                                                         scalar=float(width), in1=cnt[:, :],
                                                         op0=ALU.mult, op1=ALU.add))

                per = 2 * (4 if middle else 3)
                for h in range(2):
                    stage_rows(slice(h * SHALF, (h + 1) * SHALF), h)
                first = st.now()
                with v.Fori(0, SITER - 1) as it:
                    st.at(it * per + first)
                    for h in range(2):
                        v.wait_ge(got_sem[h], 16 * SHALF * (it + 1))
                        count(bass.ds(it * (2 * SHALF) + h * SHALF, SHALF), h)
                        stage_rows(bass.ds(it * (2 * SHALF) + (2 + h) * SHALF, SHALF), h)
                    assert st.n == per
                st.at(first + per * (SITER - 1))
                for h in range(2):
                    v.wait_ge(got_sem[h], 16 * SHALF * SITER)
                    at = (2 * (SITER - 1) + h) * SHALF
                    count(slice(at, at + SHALF), h)

            search(row2, s_idx2, s_got2, got2, SEARCH_ROW2, row3)
            search(row3, s_idx3, s_got3, got3, SEARCH_ROW3, start)

            st.done(v.tensor_copy(rec[:, :, 0], q_i[:, 0:T]))
            st.done(v.tensor_copy(rec[:, :, 1], start[:, 0:T]))
            st.link(v.tensor_tensor(cols[:, :], start[:, 1:T + 1], start[:, 0:T], ALU.subtract))
            st.done(v.tensor_copy(rec[:, :, 2], cols[:, :]))
            st.link(v.tensor_scalar(bins[:, :], cols[:, :], float(BINS - 1), -1.0, ALU.min, ALU.mult))
            st.link(v.tensor_scalar(bins[:, :], bins[:, :], float(BINS - 1), None, ALU.add))
            st.link(v.tensor_copy(bin_b[:, :], bins[:, :]))
            st.link(v.tensor_tensor(onehot[:, :, :], bc_mid(iota_bin[:, :], T), bc(bins[:, :], BINS), ALU.is_equal))
            v.tensor_reduce(bin_tot[:, :], onehot[:, :, :].rearrange("p t b -> p b t"), AX.X, ALU.add).then_inc(s_bins, 1)
            v.tensor_tensor(pairs, bc_mid(bin_b[:, :], T), bc(bin_b[:, :], T), ALU.is_equal).then_inc(s_pair, 1)
            v.wait_ge(s_const, 5)
            st.link(v.tensor_reduce(cols2[:, :], pairs, AX.X, ALU.add))
            v.wait_ge(s_binp, 1)
            st.link(v.tensor_copy(bin_tot[:, :], ps_t[:, 0:BINS]))
            st.link(v.tensor_tensor_scan(bin_scan[:, :], ones[:, 0:BINS], bin_tot[:, :], 0.0, ALU.mult, ALU.add))
            st.link(v.tensor_tensor(bin_scan[:, :], bin_scan[:, :], bin_tot[:, :], ALU.subtract))
            st.link(v.tensor_tensor(bin_off[:, :], bin_scan[:, :], ps_u[:, 0:BINS], ALU.add))
            st.link(v.tensor_tensor(onehot[:, :, :], onehot[:, :, :], bc_mid(bin_off[:, :], T), ALU.mult))
            st.link(v.tensor_reduce(cols3[:, :], onehot[:, :, :], AX.X, ALU.add))
            st.link(v.tensor_tensor(cols2[:, :], cols2[:, :], cols3[:, :], ALU.add))
            st.link(v.tensor_copy(icols[:, :], cols2[:, :]))
            st.done(v.tensor_single_scalar(icols2[:, :], icols[:, :], P - 1, ALU.bitwise_and))
            st.link(v.tensor_single_scalar(icols[:, :], icols[:, :], P.bit_length() - 1, ALU.logical_shift_right))
            st.done(v.tensor_copy(cols2[:, :], icols2[:, :]))
            st.link(v.tensor_copy(cols3[:, :], icols[:, :]))
            st.link(v.scalar_tensor_tensor(out=cols[:, :], in0=cols2[:, :], scalar=float(T), in1=cols3[:, :],
                                           op0=ALU.mult, op1=ALU.add))
            st.link(v.tensor_copy(rec[:, :, 4], cols[:, :]))

            def stage_record(tiles_at, h):
                v.tensor_copy(rank_rec[:, h, :, :], rec[:, tiles_at, :]).then_inc(s_rec, 1)

            for h in range(2):
                stage_record(slice(h * THALF, (h + 1) * THALF), h)
            with v.Fori(0, TITER - 1) as it:
                for h in range(2):
                    wait_alone(v, s_recw[h], 16 * THALF * (it + 1))
                    stage_record(bass.ds(it * (2 * THALF) + (2 + h) * THALF, THALF), h)

            def layer_norm_relu(rows, to, scratch, count):
                st.link(v.tensor_reduce(cols[:, :], rows, AX.X, ALU.add))
                st.link(v.tensor_scalar(cols[:, :], cols[:, :], 1.0 / D, None, ALU.mult))
                st.link(v.tensor_tensor(to, rows, bc(cols[:, :], D), ALU.subtract))
                st.link(v.tensor_tensor(scratch, to, to, ALU.mult))
                v.tensor_reduce(cols2[:, :], scratch, AX.X, ALU.add).then_inc(s_var, 1)
                v.wait_ge(s_std, count)
                st.link(v.reciprocal(cols3[:, :], cols3[:, :]))
                st.link(v.tensor_tensor(to, to, bc(cols3[:, :], D), ALU.mult))
                return v.tensor_scalar(to, to, 0.0, None, ALU.max)

            v.wait_ge(s_x, X_DMAS)
            layer_norm_relu(x_nodes, h_nodes, hr[:, :, :], 1).then_inc(s_h0, 1)

            v.wait_ge(s_rank, 16)
            st.link(v.tensor_copy(deg[:, :], ranked[:, :, 2]))
            v.tensor_scalar(rdeg[:, :], deg[:, :], 1.0, None, ALU.max).then_inc(s_degf, 1)
            v.wait_ge(s_degf, 1)
            st.link(v.reciprocal(rdeg[:, :], rdeg[:, :]))
            v.wait_ge(s_degT, 1)
            v.tensor_reduce(cols[0:T, 0:1], ps_y[0:T, 0:P], AX.X, ALU.max).then_inc(s_mxc, 1)
            v.wait_ge(s_mxr, 1)
            st.link(v.tensor_copy(irow[:, 0, :], ps_h[0:1, 0:T]))
            st.link(v.tensor_copy(crow[:, 0, :], ps_h[0:1, 0:T]))
            for at, unit in ((1, SLOTS), (2, RUN)):
                st.link(v.tensor_scalar(crow[:, 3, :], crow[:, 0, :], float(unit - 1), None, ALU.add))
                st.link(v.tensor_copy(irow[:, 3, :], crow[:, 3, :]))
                st.link(v.tensor_single_scalar(irow[:, at, :], irow[:, 3, :], unit.bit_length() - 1,
                                               ALU.logical_shift_right))
                st.link(v.tensor_copy(crow[:, at, :], irow[:, at, :]))
                st.link(v.tensor_scalar(crow[:, at, :], crow[:, at, :], 2.0 if at == 1 else 1.0, None, ALU.max))
                st.link(v.tensor_copy(ctl[:, :, 2 * at - 2], crow[:, at, :]))
                st.link(v.tensor_tensor_scan(crow[:, 3, :], one1[:, :], crow[:, at, :], 0.0, ALU.mult, ALU.add))
                if at == 1:
                    st.link(v.tensor_copy(tot[:, 0:1], crow[:, 3, T - 1:T]))
                    st.link(v.tensor_scalar(cols[0:1, 1:2], crow[:, 3, T - 1:T], float(RING - 1), None, ALU.add))
                    st.link(v.tensor_copy(tot[:, 1:2], cols[0:1, 1:2]))
                    st.link(v.tensor_single_scalar(tot[:, 3:4], tot[:, 1:2], RING.bit_length() - 1,
                                                   ALU.logical_shift_right))
                    st.link(v.tensor_copy(tot[:, 1:2], tot[:, 3:4]))
                else:
                    st.link(v.tensor_scalar(cols[0:1, 1:2], crow[:, 3, T - 1:T], float(-T), None, ALU.add))
                    st.link(v.tensor_copy(tot[:, 2:3], cols[0:1, 1:2]))
                st.link(v.tensor_tensor(crow[:, 3, :], crow[:, 3, :], crow[:, at, :], ALU.subtract))
                v.tensor_copy(ctl[:, :, 2 * at - 1], crow[:, 3, :]).then_inc(s_ctl, 1)
                v.wait_ge(s_ctl, at)

            def mask(got, to, rest, steps, scratch):
                steps.link(v.tensor_tensor(scratch[0], scratch[1], rest, ALU.is_lt))
                steps.link(v.scalar_tensor_tensor(out=scratch[0], in0=got, scalar=float(-ZROW), in1=scratch[0],
                                                  op0=ALU.add, op1=ALU.mult))
                return v.tensor_scalar(to, scratch[0], float(ZROW), None, ALU.add)

            gen = Steps(v, s_gen, wait_alone)
            offset, left = cols2[:, 0:1], cols2[:, 1:2]
            with v.If(extra_blocks(v) > 0):
                with v.Fori(0, T) as i:
                    n, before = tile_blocks(v, i)
                    gen.at((before * 4) + (i * 2))
                    gen.done(v.tensor_copy(offset, at_tile(ranked, i, 1, 2)))
                    gen.link_alone(v.tensor_copy(left, at_tile(ranked, i, 2, 3)))
                    with v.Fori(0, n) as b:
                        gen.at((before + b) * 4 + (i * 2 + 2))
                        v.tensor_scalar(tstage[:, 0, 0, 1:2], offset, float(E), None, ALU.min).then_inc(s_blk, 1)
                        v.wait_ge(s_blkl, (before + b + 1) * 16)
                        v.wait_ge(s_blk, before + b + 1)
                        mask(runs[:, 0, 0, :], runs_m[:, 0, 0, :], left.to_broadcast([P, RUN]), gen,
                             (valid[:, 0, :], iota_run[:, :])).then_inc(s_blkm, 1)
                        gen.done(v.tensor_scalar(offset, offset, float(RUN), None, ALU.add))
                        gen.link(v.tensor_scalar(left, left, float(-RUN), None, ALU.add))
                        wait_alone(v, s_blkm, before + b + 1)
                        wait_alone(v, s_blkw, (before + b + 1) * 16)
                        v.nop()

            def stage_tiles(tiles_at, h):
                v.tensor_copy(tstage[:, h, :, :], ranked[:, tiles_at, 0:2]).then_inc(s_tidx, 1)

            def take_tiles(tiles_at, h):
                st.link(v.tensor_copy(xr[:, tiles_at, :], xland[:, h, :, :]))
                mask(runs[:, h, :, :], runs_m[:, h, :, :], bc(deg[:, tiles_at], RUN), st,
                     (valid[:, :, :], bc_mid(iota_run[:, :], THALF))).then_inc(s_mask, 1)

            for h in range(2):
                stage_tiles(slice(h * THALF, (h + 1) * THALF), h)
            first, per = st.now(), 2 * 3

            def tiles_of(it, h):
                wait_alone(v, s_land[h], 32 * THALF * (it + 1))
                wait_alone(v, s_rfree, 2 * it + h + 1)
                take_tiles(bass.ds(it * (2 * THALF) + h * THALF, THALF), h)

            with v.Fori(0, TITER - 1) as it:
                st.at(it * per + first)
                for h in range(2):
                    tiles_of(it, h)
                    wait_alone(v, s_mask, 2 * it + h + 1)
                    stage_tiles(bass.ds(it * (2 * THALF) + (2 + h) * THALF, THALF), h)
                assert st.n == per
            st.at(first + per * (TITER - 1))
            for h in range(2):
                tiles_of(TITER - 1, h)

            v.wait_ge(s_tab, TAB_DMAS)
            v.wait_ge(s_h0w, 32)
            layer_norm_relu(xr[:, :, :], hr[:, :, :], x_nodes, 2).then_inc(s_hr, 1)
            v.wait_ge(s_hr, 1)

            first, per = st.now(), 6
            with v.Fori(0, T) as i:
                st.at(i * per + first)
                v.wait_ge(l0.sum, i + 1)
                v.tensor_scalar(cat[:, D:2 * D], ps_sum[:, 0:D], rdeg[:, bass.ds(i, 1)], None,
                                ALU.mult).then_inc(l0.cat, 1)
                v.tensor_copy(cat[:, 0:D], at_tile(hr, i)).then_inc(l0.cat, 1)
                v.wait_ge(l0.y, i + 1)
                st.link_alone(v.scalar_tensor_tensor(out=at_tile(xr, i), in0=ps_y[:, 0:D], scalar=0.0,
                                                     in1=at_tile(xr, i), op0=ALU.max, op1=ALU.add))
                st.link_alone(v.bn_stats(stats[:, :], at_tile(xr, i)))
                v.bn_aggr(mv[:, :], stats[:, :]).then_inc(s_var1, 1)
                v.wait_ge(s_std1, i + 1)
                st.link(v.reciprocal(rstd[:, :], std[:, :]))
                v.wait_ge(s_row, 16 * (i + 1))
                st.link(v.tensor_scalar(rowbuf[:, 0:D], at_tile(xr, i), mv[:, 0:1], rstd[:, 0:1],
                                        ALU.subtract, ALU.mult))
                v.tensor_scalar(rowbuf[:, 0:D], rowbuf[:, 0:D], 0.0, None, ALU.max).then_inc(s_h1, 1)
                wait_alone(v, s_h1, i + 1)
                st.done(v.tensor_copy(at_tile(hr, i), rowbuf[:, 0:D]))
                st.link_alone(v.tensor_copy(rowbuf[:, WROW:WROW + 1].bitcast(I32), at_tile(ranked, i, 0, 1)))
                wait_alone(v, s_ab, i + 1)
                v.tensor_copy(at_tile(b_self, i), ps_h[:, 0:H]).then_inc(l0.tile, 1)
                assert st.n == per
            st.at(first + per * T)

            v.wait_ge(l0.tile, T)
            first = st.now()

            def pre_act(w, i):
                v.wait_ge(l1.landed, w + 1)
                rows = ring1[:, bass.ds(w & (RING - 1), 1), :, :].rearrange("p c s w -> p (c s) w")
                v.tensor_tensor(pre[:, :, :], rows[:, :, D:WROW],
                                b_self[:, bass.ds(i, 1), :].to_broadcast([P, SLOTS, H]), ALU.add).then_inc(s_pre, 1)

            def weigh(w):
                v.wait_ge(s_pre, w + 1)
                v.scalar_tensor_tensor(out=act_w[:, :, :], in0=pre[:, :, :], scalar=0.0,
                                       in1=bc_mid(we2_rows[:, :], SLOTS), op0=ALU.max, op1=ALU.mult).then_inc(s_act, 1)

            def score(w):
                v.wait_ge(s_act, w + 1)
                v.tensor_reduce(z[:, :], act_w[:, :, :], AX.X, ALU.add).then_inc(s_z, 1)

            def message(w):
                v.wait_ge(s_gate, w + 1)
                v.wait_ge(s_msgf, w + 1)
                rows = ring1[:, bass.ds(w & (RING - 1), 1), :, :].rearrange("p c s w -> p (c s) w")
                v.tensor_tensor(msg[:, :, :], rows[:, :, 0:D], bc(gate[:, :], D), ALU.mult).then_inc(s_msg, 1)

            def chunk_maximum(w):
                v.wait_ge(s_msg, w + 1)
                v.wait_ge(s_acc, w + 1)
                v.tensor_reduce(chunk_max[:, :], msg[:, :, :].rearrange("p s d -> p d s"), AX.X,
                                ALU.max).then_inc(l1.used, 1)

            def maximum(w):
                v.wait_ge(l1.used, w + (RING + 1))
                v.tensor_tensor(cat[:, 0:D], cat[:, 0:D], chunk_max[:, :], ALU.max).then_inc(s_acc, 1)

            def finish(i):
                v.wait_ge(l1.y, i + 1)
                st.link(v.tensor_tensor(rowbuf[:, 0:D], ps_y[:, 0:D], at_tile(hr, i), ALU.add))
                st.done(v.tensor_tensor(at_tile(xr, i), rowbuf[:, 0:D], at_tile(xr, i), ALU.add))

            def tile(i, before_it):
                n, before = tile_counts(v, i)
                if before_it is not None:
                    wait_alone(v, l1.catT, i)
                st.link_alone(v.memset(cat[:, 0:D], 0.0))
                w = v.snap(before + 0)
                pre_act(w, i)
                weigh(w)
                score(w)
                if before_it is not None:
                    finish(before_it)
                with v.Fori(1, n) as c:
                    w = v.snap(before + c)
                    last = v.snap(w - 1)
                    pre_act(w, i)
                    message(last)
                    weigh(w)
                    chunk_maximum(last)
                    score(w)
                    maximum(last)
                last = v.snap(before + n - 1)
                message(last)
                chunk_maximum(last)
                maximum(last)
                wait_alone(v, l1.sum, i + 1)
                v.tensor_copy(h_tile[:, :], at_tile(hr, i)).then_inc(l1.cat, 1)
                v.tensor_copy(cat[:, D:2 * D], ps_sum[:, 0:D]).then_inc(l1.cat, 1)

            v.sem_inc(s_acc, 1)
            tile(0, None)
            first, per = st.now(), 3
            with v.Fori(1, T) as i:
                st.at(i * per + (first - per))
                tile(i, i - 1)
                assert st.n == per
            st.at(first + per * (T - 1))
            finish(T - 1)
            st.wait()


            def stage_out(tiles_at, h):
                v.tensor_copy(out_rows[:, h, :, :], xr[:, tiles_at, :]).then_inc(s_outs, 1)
                v.tensor_copy(out_idx[:, h, :, :], ranked[:, tiles_at, 0:2]).then_inc(s_outs, 1)

            for h in range(2):
                stage_out(slice(h * THALF, (h + 1) * THALF), h)
            with v.Fori(0, TITER - 1) as it:
                for h in range(2):
                    wait_alone(v, s_outw[h], 16 * THALF * (it + 1))
                    stage_out(bass.ds(it * (2 * THALF) + (2 + h) * THALF, THALF), h)

        @block.scalar
        def _(act):
            def load(to, frm):
                act.dma_start(to, frm).then_inc(s_w, 16)

            load(w_cat[0:D, :], w_self[:, :])
            load(w_cat[D:2 * D, :], w_neigh[:, :])
            load(w_ab[:, 0:H], we1[0:D, :])
            load(w_ab[:, H:2 * H], we1[D:2 * D, :])
            load(w_n1a[:, :], wn1[0:2 * D, :])
            load(w_n1b[:, :], wn1[2 * D:3 * D, :])
            load(w_n2[:, :], wn2[:, :])
            load(b0_row[:, :], b0[:].unsqueeze(0))
            load(bn2_row[:, :], bn2[:].unsqueeze(0))
            load(bn1_col[:, :], bn1[:].unsqueeze(1))
            load(be2_col[:, :], be2[:].unsqueeze(0).to_broadcast([P, 1]))
            load(we2_rows[:, :], we2.rearrange("h a -> a h").to_broadcast([P, H]))
            act.wait_ge(s_zero, 2)
            load(be1_row[:, :], be1[:].unsqueeze(0))
            act.dma_start(h0_table[ZROW:ZROW + 1, :], zeros[0:1, 0:D]).then_inc(s_h0w, 16)
            act.dma_start(hA_table[ZROW:ZROW + 1, :], zeros[0:1, :]).then_inc(s_row, 16)

            act.wait_ge(s_var, 1)
            act.activation(cols3[:, :], cols2[:, :], ACT.Sqrt, bias=eps_col[:, 0:1], scale=1.0 / D).then_inc(s_std, 1)
            act.wait_ge(s_h0, 1)
            act.dma_start(h0_table[0:NP, :].rearrange("(p t) d -> p t d", p=P), h_nodes).then_inc(s_h0w, 16)
            act.wait_ge(s_var, 2)
            act.activation(cols3[:, :], cols2[:, :], ACT.Sqrt, bias=eps_col[:, 0:1], scale=1.0 / D).then_inc(s_std, 1)

            act.wait_ge(s_w, W_DMAS)
            with act.Fori(0, T) as i:
                act.wait_ge(l0.catT, i + 1)
                act.activation(catT[:, :], ps_t[:, 0:P], ACT.Copy).then_inc(l0.catTs, 1)
                act.wait_ge(s_var1, i + 1)
                act.activation(std[:, :], mv[:, 1:2], ACT.Sqrt, bias=eps_col[:, 0:1]).then_inc(s_std1, 1)
                act.wait_ge(s_h1T, i + 1)
                act.activation(hT[:, :], ps_u[0:D, 0:P], ACT.Copy).then_inc(s_h1Ts, 1)
                act.wait_ge(s_ab, i + 1)
                act.activation(rowbuf[:, D:WROW], ps_a[:, 0:H], ACT.Copy).then_inc(s_rowA, 1)
                act.wait_ge(s_rowA, i + 1)
                act.wait_ge(l0.tile, i + 1)
                act.dma_start(ranked_rows[:, bass.ds(i * (WROW + 1), WROW + 1)], rowbuf[:, :]).then_inc(s_row, 16)

            with act.Fori(0, T) as i:
                n, before = tile_counts(act, i)
                with act.Fori(0, n) as c:
                    w = act.snap(before + c)
                    act.wait_ge(s_z, w + 1)
                    act.activation(gate[:, :], z[:, :], ACT.Sigmoid, bias=be2_col[:, 0:1]).then_inc(s_gate, 1)
                act.wait_ge(l1.catT, i + 1)
                act.activation(catT[:, :], ps_t[:, 0:P], ACT.Copy).then_inc(l1.catTs, 1)
                act.activation(hT[:, :], ps_u[0:D, 0:P], ACT.Copy).then_inc(l1.catTs, 1)
                act.wait_ge(s_hid, i + 1)
                act.activation(h2T[:, :], ps_h[:, 0:P], ACT.Relu, bias=bn1_col[:, 0:1]).then_inc(s_hids, 1)

        @block.tensor
        def _(pe):
            pe.wait_ge(s_const, 4)
            pe.wait_ge(s_bins, 1)
            pe.matmul(ps_t[:, 0:BINS], ones[:, :], bin_tot[:, :], start=True, stop=True)
            pe.matmul(ps_u[:, 0:BINS], upper[:, :], bin_tot[:, :], start=True, stop=True).then_inc(s_binp, 1)
            pe.wait_ge(s_degf, 1)
            pe.transpose(ps_y[0:T, 0:P], deg[:, :], ident[:, :]).then_inc(s_degT, 1)
            pe.wait_ge(s_mxc, 1)
            pe.transpose(ps_h[0:1, 0:T], cols[0:T, 0:1], ident[0:T, 0:T]).then_inc(s_mxr, 1)
            pe.wait_ge(s_ctl, 2)
            pe.wait_ge(s_w, W_DMAS)

            def sum_start():
                pe.matmul(ps_sum[:, 0:D], zeros[0:1, 0:P], zeros[0:1, 0:D], start=True, stop=False,
                          skip_group_check=True)

            def sum_add(rows):
                return pe.matmul(ps_sum[:, 0:D], ident[:, :], rows, start=False, stop=False, skip_group_check=True)

            def sum_stop():
                return pe.matmul(ps_sum[:, 0:D], zeros[0:1, 0:P], zeros[0:1, 0:D], start=False, stop=True,
                                 skip_group_check=True)

            pe.sem_inc(l0.used, RING)
            with pe.Fori(0, T) as i:
                n, before = tile_counts(pe, i)
                sum_start()
                with pe.Fori(0, n) as c:
                    w = pe.snap(before + c)
                    place = pe.snap(w & (RING - 1))
                    pe.wait_ge(l0.landed, w + 1)
                    for s in range(SLOTS):
                        last = sum_add(ring0[:, bass.ds(place, 1), s, :].rearrange("p c w -> p (c w)"))
                    last.then_inc(l0.used, 1)
                sum_stop().then_inc(l0.sum, 1)
                pe.wait_ge(l0.cat, 2 * i + 2)
                pe.transpose(ps_t[:, 0:P], cat[:, :], ident[:, :]).then_inc(l0.catT, 1)
                pe.wait_ge(l0.catTs, i + 1)
                pe.matmul(ps_y[:, 0:D], catT[:, :], w_cat[:, :], start=True, stop=False)
                pe.matmul(ps_y[:, 0:D], ones[0:1, 0:P], b0_row[:, :], start=False, stop=True).then_inc(l0.y, 1)
                wait_alone(pe, s_h1, i + 1)
                pe.transpose(ps_u[0:D, 0:P], rowbuf[:, 0:D], ident[:, :]).then_inc(s_h1T, 1)
                pe.wait_ge(s_h1Ts, i + 1)
                pe.matmul(ps_a[:, 0:H], hT[:, :], w_ab[:, 0:H], start=True, stop=True)
                pe.matmul(ps_h[:, 0:H], hT[:, :], w_ab[:, H:2 * H], start=True, stop=False)
                pe.matmul(ps_h[:, 0:H], ones[0:1, 0:P], be1_row[:, :], start=False, stop=True).then_inc(s_ab, 1)

            pe.sem_inc(l1.used, RING)
            pe.sem_inc(s_msgf, 1)
            with pe.Fori(0, T) as i:
                n, before = tile_counts(pe, i)
                sum_start()
                with pe.Fori(0, n) as c:
                    w = pe.snap(before + c)
                    pe.wait_ge(s_msg, w + 1)
                    for s in range(SLOTS):
                        last = sum_add(msg[:, s, :])
                    last.then_inc(s_msgf, 1)
                sum_stop().then_inc(l1.sum, 1)
                wait_alone(pe, l1.cat, 2 * i + 2)
                pe.transpose(ps_u[0:D, 0:P], h_tile[:, :], ident[:, :])
                pe.transpose(ps_t[:, 0:P], cat[:, :], ident[:, :]).then_inc(l1.catT, 1)
                pe.wait_ge(l1.catTs, 2 * i + 2)
                pe.matmul(ps_h[:, 0:P], w_n1a[:, :], catT[:, :], start=True, stop=False)
                pe.matmul(ps_h[:, 0:P], w_n1b[:, :], hT[:, :], start=False, stop=True).then_inc(s_hid, 1)
                pe.wait_ge(s_hids, i + 1)
                pe.matmul(ps_y[:, 0:D], h2T[:, :], w_n2[:, :], start=True, stop=False)
                pe.matmul(ps_y[:, 0:D], ones[0:1, 0:P], bn2_row[:, :], start=False, stop=True).then_inc(l1.y, 1)


_INS = ['x', 'src', 'dst', 'L0_gnn_W_self', 'L0_gnn_W_neigh', 'L0_gnn_b', 'L1_gnn_We1', 'L1_gnn_be1', 'L1_gnn_We2',
        'L1_gnn_be2', 'L1_gnn_Wn1', 'L1_gnn_bn1', 'L1_gnn_Wn2', 'L1_gnn_bn2']


def kernel(**inputs):
    import numpy as _np
    import concourse.bacc as _bacc
    from concourse import mybir as _mybir
    from concourse.bass_utils import run_bass_kernel_spmd as _run

    nc = _bacc.Bacc("TRN2", target_bir_lowering=False, num_devices=1)
    arrays, args = {}, []
    for name in _INS:
        a = _np.ascontiguousarray(inputs[name])
        arrays[f"in_{name}_dram"] = a
        args.append(nc.dram_tensor(f"in_{name}_dram", a.shape, _mybir.dt.from_np(a.dtype), kind="ExternalInput").ap())
    args.append(nc.dram_tensor("out_dram", inputs['x'].shape, _mybir.dt.float32, kind="ExternalOutput").ap())
    gnn_kernel(nc, *args)
    r = _run(nc, [arrays], core_ids=[0])
    return r.results[0]["out_dram"]
```

```python
from contextlib import ExitStack

import concourse.bass as bass
from concourse import mybir

F32 = mybir.dt.float32
BF16 = mybir.dt.bfloat16
I32 = mybir.dt.int32
ALU = mybir.AluOpType
ACT = mybir.ActivationFunctionType
AX = mybir.AxisListType

P = 128
EPS = 1e-5

SLOTS = 4
STAGES = 2
STAGE_COLS = 16
GROUP_COLS = STAGES * STAGE_COLS
RING = GROUP_COLS // SLOTS
STAGE_CHUNKS = STAGE_COLS // SLOTS

RUN = 64
BINS = 64
PARTS = 5
PCOLS = 2
REC = 4


class Steps:

    def __init__(self, eng, sem, alone):
        self.eng, self.sem, self.alone, self.base, self.n = eng, sem, alone, 0, 0

    def done(self, ins):
        ins.then_inc(self.sem, 1)
        self.n += 1

    def wait(self):
        self.eng.wait_ge(self.sem, self.base + self.n)

    def link(self, ins):
        self.done(ins)
        self.wait()

    def link_alone(self, ins):
        self.done(ins)
        self.alone(self.eng, self.sem, self.base + self.n)

    def at(self, base):
        self.base, self.n = base, 0

    def now(self):
        return self.base + self.n


def gnn_kernel(nc, x, src, dst, w_self, w_neigh, b0, we1, be1, we2, be2, wn1, bn1, wn2, bn2, out):
    N, D = x.shape
    E = src.shape[0]
    H = we1.shape[1]
    T = -(-N // P)
    NP = T * P
    ZROW = NP
    NROWS = NP + 1
    FULL = N // T
    REST = N - FULL * T

    ROW = max(r for r in range(1, T * D // (PARTS * PCOLS) + 1) if E % r == 0)
    TOP = E // ROW
    PASS = PARTS * PCOLS
    SITER = -(-(T + 1) // PASS)
    SCOLS = SITER * PASS
    THALF = 7
    TITER = T // (2 * THALF)
    assert TITER * 2 * THALF == T and T <= P

    SRC_ROWS = -(-(E + RUN) // RUN)
    SRC_PAD = SRC_ROWS * RUN - E
    MAXCOLS = E + 2 * T * SLOTS
    MAXCHUNKS = MAXCOLS // SLOTS
    MAXBLOCKS = E // RUN + T + 1
    STREAM = (MAXCOLS // RUN + 3 + THALF) * RUN

    def dram(name, shape, dt):
        return nc.dram_tensor(name, shape, dt).ap()

    dst_rows = dst.rearrange("(a b) -> a b", b=ROW)
    dst_top = dram("dst_top", (TOP,), I32)
    src_pad = dram("src_pad", (SRC_ROWS, RUN), I32)
    h0_table = dram("h0_table", (NROWS, D), F32)
    records = dram("records", (NP, D + REC), F32)
    stream = dram("stream", (P, STREAM), I32)
    WROW = D + H
    ranked_rows = dram("ranked_rows", (P, T * (WROW + 1)), F32)
    hA_table = dram("hA_table", (NROWS, WROW), F32)

    with ExitStack() as ctx:
        def sb(name, shape, dt=F32):
            return ctx.enter_context(nc.sbuf_tensor(name, shape, dt))

        def psum(name, shape):
            return ctx.enter_context(nc.psum_tensor(name, shape, F32))

        def sem(name):
            return ctx.enter_context(nc.semaphore(name))

        ident = sb("ident", [P, P])
        upper = sb("upper", [P, P])
        ones = sb("ones", [P, P])
        w_cat = sb("w_cat", [2 * D, D])
        w_ab = sb("w_ab", [D, 2 * H])
        w_n1a = sb("w_n1a", [2 * D, H])
        w_n1b = sb("w_n1b", [D, H])
        w_n2 = sb("w_n2", [H, D])
        b0_row = sb("b0_row", [1, D])
        be1_row = sb("be1_row", [1, H])
        bn2_row = sb("bn2_row", [1, D])
        bn1_col = sb("bn1_col", [H, 1])
        be2_col = sb("be2_col", [P, 1])
        eps_col = sb("eps_col", [P, 1])
        we2_rows = sb("we2_rows", [P, H])
        src_tail = sb("src_tail", [1, SRC_PAD], I32)
        zeros = sb("zeros", [P, WROW])
        zcols = sb("zcols", [P, RUN], I32)

        rec = sb("rec", [P, T, REC + 1], I32)
        by_rank = sb("by_rank", [P, T, D + REC])
        xr = by_rank[:, :, 0:D]
        ranked = by_rank[:, :, :].bitcast(I32)[:, :, D:D + REC]
        deg = sb("deg", [P, T])
        rdeg = sb("rdeg", [P, T])
        ctl = sb("ctl", [1, T, 5], I32)
        tot = sb("tot", [1, 4], I32)
        hr = sb("hr", [P, T, D])
        b_self = sb("b_self", [P, T, H])
        ring = sb("ring", [P, GROUP_COLS * WROW])
        stage = sb("stage", [P, STAGES, STAGE_COLS], I32)

        x_nodes = b_self[:, :, 0:D]
        h_nodes = b_self[:, :, D:2 * D]
        onehot = hr

        q = sb("q", [P, SCOLS])
        q_mid = sb("q_mid", [P, SCOLS])
        top = sb("top", [P, TOP])
        top_i = sb("top_i", [P, TOP], I32)
        junk = sb("junk", [P, PASS, TOP], BF16)
        junk2 = sb("junk2", [P, PCOLS, ROW], BF16)
        balance = sb("balance", [P, SCOLS])
        row = sb("row", [P, SCOLS])
        below = sb("below", [P, SCOLS])
        start = sb("start", [P, SCOLS])
        sstage = sb("sstage", [P, PARTS, PCOLS], I32)
        cols = sb("cols", [P, T])
        cols2 = sb("cols2", [P, T])
        cols3 = sb("cols3", [P, T])
        icols = sb("icols", [P, T], I32)
        icols2 = sb("icols2", [P, T], I32)
        top_deg = sb("top_deg", [P, 1])
        bins = sb("bins", [P, T])
        bin_b = sb("bin_b", [P, T], BF16)
        iota_bin = sb("iota_bin", [P, BINS])
        iota_run = sb("iota_run", [P, RUN])
        iota_i = sb("iota_i", [P, RUN], I32)
        q_i = sb("q_i", [P, SCOLS], I32)
        bin_tot = sb("bin_tot", [P, BINS])
        bin_scan = sb("bin_scan", [P, BINS])
        bin_off = sb("bin_off", [P, BINS])
        rank_rec = sb("rank_rec", [P, 2, THALF, D + REC + 1])
        tstage = sb("tstage", [P, 2, THALF, 2], I32)
        out_rows = sb("out_rows", [P, 2, THALF, D])
        runs = sb("runs", [P, 2, THALF, RUN], I32)
        runs_m = sb("runs_m", [P, 2, THALF * RUN], I32)
        merge_max = sb("merge_max", [1, T], I32)
        valid = sb("valid", [P, THALF, RUN])
        crow = sb("crow", [1, 4, T])
        irow = sb("irow", [1, 4, T], I32)
        cols_row = sb("cols_row", [1, T])
        one1 = sb("one1", [1, T])

        cat = sb("cat", [P, 2 * D])
        catT = sb("catT", [P, P])
        hT = sb("hT", [D, P])
        h_tile = sb("h_tile", [P, D])
        h2T = sb("h2T", [H, P])
        rowbuf = sb("rowbuf", [P, WROW + 1])
        stats = sb("stats", [P, 6])
        mv = sb("mv", [P, 2])
        std = sb("std", [P, 1])
        rstd = sb("rstd", [P, 1])
        pre = sb("pre", [P, SLOTS, H])
        act_w = sb("act_w", [P, SLOTS, H])
        z = sb("z", [P, SLOTS])
        gate = sb("gate", [P, SLOTS])
        msg = sb("msg", [P, SLOTS, D])
        chunk_max = sb("chunk_max", [P, D])

        pairs = ring[:, 0:T * T // 2 + 1].bitcast(BF16)[:, 0:T * T].rearrange("p (a b) -> p a b", a=T)
        got = hr[:, :, :].rearrange("p t d -> p (t d)")[:, 0:PASS * ROW].bitcast(I32).rearrange(
            "p (a b r) -> p a b r", a=PARTS, b=PCOLS)
        fin_rows = ring[:, 0:2 * THALF * (WROW + 1)].rearrange("p (h t w) -> p h t w", h=2, t=THALF)
        ring0 = ring[:, 0:GROUP_COLS * D].rearrange("p (c s w) -> p c s w", c=RING, s=SLOTS)
        ring1 = ring[:, :].rearrange("p (c s w) -> p c s w", c=RING, s=SLOTS)
        out_idx = tstage

        ps_sum = psum("ps_sum", [P, 512])
        ps_t = psum("ps_t", [P, 512])
        ps_u = psum("ps_u", [P, 512])
        ps_y = psum("ps_y", [P, 512])
        ps_a = psum("ps_a", [P, 512])
        ps_h = psum("ps_h", [P, 512])

        s_passed = sem("s_passed")
        s_const = sem("s_const")
        s_zero = sem("s_zero")
        s_topd = sem("s_topd")
        s_top = sem("s_top")
        s_w = sem("s_w")
        s_x = sem("s_x")
        s_tab = sem("s_tab")
        s_dve = sem("s_dve")
        s_q = sem("s_q")
        s_bal = sem("s_bal")
        s_idx = sem("s_idx")
        s_got = [sem(f"s_got{a}") for a in range(PARTS)]
        s_bins = sem("s_bins")
        s_binp = sem("s_binp")
        s_pair = sem("s_pair")
        s_gen = sem("s_gen")
        s_rfree = sem("s_rfree")
        s_rec = sem("s_rec")
        s_recw = [sem(f"s_recw{h}") for h in range(2)]
        s_rank = sem("s_rank")
        s_var = sem("s_var")
        s_std = sem("s_std")
        s_h0 = sem("s_h0")
        s_h0w = sem("s_h0w")
        s_degf = sem("s_degf")
        s_degT = sem("s_degT")
        s_mxc = sem("s_mxc")
        s_mxr = sem("s_mxr")
        s_ctl = sem("s_ctl")
        s_tidx = sem("s_tidx")
        s_land = [sem(f"s_land{h}") for h in range(2)]
        s_mask = sem("s_mask")
        s_wr = sem("s_wr")
        s_blk = sem("s_blk")
        s_blkl = sem("s_blkl")
        s_blkm = sem("s_blkm")
        s_blkw = sem("s_blkw")
        s_free = sem("s_free")
        s_stream = sem("s_stream")
        s_hr = sem("s_hr")

        class Layer:
            def __init__(self, n):
                self.staged = [sem(f"s_staged{n}_{h}") for h in range(STAGES)]
                self.got = [sem(f"s_got{n}_{c}") for c in range(RING)]
                self.landed = sem(f"s_landed{n}")
                self.used = sem(f"s_used{n}")
                self.sum = sem(f"s_sum{n}")
                self.cat = sem(f"s_cat{n}")
                self.catT = sem(f"s_catT{n}")
                self.catTs = sem(f"s_catTs{n}")
                self.y = sem(f"s_y{n}")
                self.tile = sem(f"s_tile{n}")

        l0, l1 = Layer(0), Layer(1)
        s_var1 = sem("s_var1")
        s_std1 = sem("s_std1")
        s_h1 = sem("s_h1")
        s_h1T = sem("s_h1T")
        s_h1Ts = sem("s_h1Ts")
        s_ab = sem("s_ab")
        s_rowA = sem("s_rowA")
        s_row = sem("s_row")
        s_fin = [sem(f"s_fin{h}") for h in range(2)]
        s_finw = [sem(f"s_finw{h}") for h in range(2)]
        s_pre = sem("s_pre")
        s_act = sem("s_act")
        s_acc = sem("s_acc")
        s_z = sem("s_z")
        s_gate = sem("s_gate")
        s_msg = sem("s_msg")
        s_msgf = sem("s_msgf")
        s_hid = sem("s_hid")
        s_hids = sem("s_hids")
        s_outs = sem("s_outs")
        s_outw = [sem(f"s_outw{h}") for h in range(2)]

        def tile_counts(eng, i):
            n = eng.value_load(ctl[0:1, bass.ds(i, 1), 0:1].rearrange("p a b -> p (a b)"), min_val=2, max_val=MAXCHUNKS)
            before = eng.value_load(ctl[0:1, bass.ds(i, 1), 1:2].rearrange("p a b -> p (a b)"), min_val=0, max_val=MAXCHUNKS)
            return n, before

        def groups(eng):
            return eng.value_load(tot[0:1, 1:2], min_val=1, max_val=MAXCHUNKS // RING + 1)

        def total_chunks(eng):
            return eng.value_load(tot[0:1, 0:1], min_val=T, max_val=MAXCHUNKS)

        def highest_degree(eng):
            return eng.value_load(tot[0:1, 2:3], min_val=0, max_val=E)

        def tile_blocks(eng, i):
            n = eng.value_load(ctl[0:1, bass.ds(i, 1), 2:3].rearrange("p a b -> p (a b)"), min_val=1, max_val=MAXBLOCKS)
            before = eng.value_load(ctl[0:1, bass.ds(i, 1), 3:4].rearrange("p a b -> p (a b)"), min_val=0, max_val=MAXBLOCKS)
            return n, before

        def at_tile(t, i, lo=0, hi=None):
            hi = t.shape[2] if hi is None else hi
            return t[:, bass.ds(i, 1), lo:hi].rearrange("p a b -> p (a b)")

        def wait_alone(eng, s, value):
            eng.wait_ge(s, value)
            eng.sem_inc(s_passed, 1)

        TAB_DMAS = 16 * 2
        X_DMAS = 16 * (2 if REST else 1)
        W_DMAS = 16 * 13

        block = ctx.enter_context(nc.Block())

        @block.gpsimd
        def _(pool):
            pool.iota(q_i[:, :], pattern=[[1, SCOLS]], base=0, channel_multiplier=T).then_inc(s_const, 1)
            pool.iota(iota_i[:, :], pattern=[[1, RUN]], base=0, channel_multiplier=0).then_inc(s_const, 1)
            pool.wait_ge(s_zero, 1)
            pool.affine_select(out=ident[:, :], in_=ones[:, :], compare_op=ALU.is_equal, fill=0.0, base=0,
                               pattern=[[-1, P]], channel_multiplier=1).then_inc(s_const, 1)
            pool.iota(merge_max[:, :], pattern=[[0, T // THALF], [RUN, THALF]], base=0,
                      channel_multiplier=0).then_inc(s_const, 1)
            pool.affine_select(out=upper[:, :], in_=ones[:, :], compare_op=ALU.is_gt, fill=0.0, base=0,
                               pattern=[[1, P]], channel_multiplier=-1).then_inc(s_const, 1)

            def gather(to, table, idx, axis=0):
                return pool.indirect_dma_start(to, None, table, bass.IndirectOffsetOnAxis(ap=idx, axis=axis))

            with pool.Fori(0, SITER) as it:
                for a in range(PARTS):
                    wait_alone(pool, s_idx, it * PARTS + a + 1)
                    for k in range(PCOLS):
                        gather(got[:, a, k, :], dst_rows, sstage[:, a, k:k + 1]).then_inc(s_got[a], 16)

            pool.wait_ge(s_pair, 1)
            pool.affine_select(out=pairs, in_=pairs, compare_op=ALU.is_gt, fill=0.0, base=0,
                               pattern=[[1, T], [-1, T]], channel_multiplier=0).then_inc(s_const, 1)

            with pool.Fori(0, TITER) as it:
                for h in range(2):
                    wait_alone(pool, s_rec, 4 * it + 2 * h + 2)
                    for k in range(THALF):
                        pool.indirect_dma_start(
                            records[:, :], bass.IndirectOffsetOnAxis(
                                ap=rank_rec[:, h, k, D + REC:D + REC + 1].bitcast(I32), axis=0),
                            rank_rec[:, h, k, 0:D + REC], None).then_inc(s_recw[h], 16)

            pool.wait_ge(s_tab, TAB_DMAS)
            with pool.Fori(0, TITER) as it:
                for h in range(2):
                    wait_alone(pool, s_tidx, 2 * it + h + 1)
                    for k in range(THALF):
                        gather(runs[:, h, k, :], src_pad[:, :], tstage[:, h, k, 1:2], axis=1).then_inc(s_land[h], 16)

            pool.wait_ge(s_ctl, 3)
            with pool.If(highest_degree(pool) > RUN):
                with pool.Fori(0, T) as i:
                    n, before = tile_blocks(pool, i)
                    with pool.Fori(0, n) as b:
                        wait_alone(pool, s_blk, before + b + 1)
                        gather(runs[:, 0, 0, :], src_pad[:, :], tstage[:, 0, 0, 1:2], axis=1).then_inc(s_blkl, 16)

            def gather_layer(ly, table, places, ready, ready_at):
                pool.wait_ge(ready, ready_at)
                with pool.Fori(0, groups(pool)) as g:
                    for h in range(STAGES):
                        wait_alone(pool, ly.staged[h], 16 * (g + 1))
                        for c in range(STAGE_CHUNKS * h, STAGE_CHUNKS * (h + 1)):
                            wait_alone(pool, ly.used, RING * g + c + 1)
                            for s in range(SLOTS):
                                col = (c * SLOTS + s) % STAGE_COLS
                                gather(places[:, c, s, :], table[:, :],
                                       stage[:, h, col:col + 1]).then_inc(ly.got[c], 16)

            gather_layer(l0, h0_table, ring0, s_h0w, 32)

            with pool.Fori(0, TITER) as it:
                for h in range(2):
                    wait_alone(pool, s_fin[h], 16 * (it + 1))
                    for k in range(THALF):
                        pool.indirect_dma_start(
                            hA_table[:, :],
                            bass.IndirectOffsetOnAxis(ap=fin_rows[:, h, k, WROW:WROW + 1].bitcast(I32), axis=0),
                            fin_rows[:, h, k, 0:WROW], None).then_inc(s_finw[h], 16)
            for h in range(2):
                pool.wait_ge(s_finw[h], 16 * THALF * TITER)
            gather_layer(l1, hA_table, ring1, s_row, 16)

            with pool.Fori(0, TITER) as it:
                for h in range(2):
                    wait_alone(pool, s_outs, 4 * it + 2 * h + 2)
                    for k in range(THALF):
                        pool.indirect_dma_start(
                            out[:, :], bass.IndirectOffsetOnAxis(ap=out_idx[:, h, k, 0:1], axis=0),
                            out_rows[:, h, k, :], None, bounds_check=N - 1,
                            oob_is_err=False).then_inc(s_outw[h], 16)
            for h in range(2):
                pool.wait_ge(s_outw[h], 16 * THALF * TITER)

        @block.sync
        def _(sp):
            with nc.allow_non_contiguous_dma(reason="every ROW-th entry of the sorted list"):
                sp.dma_start(dst_top[:], dst_rows[:, 0:1].rearrange("a b -> (a b)")).then_inc(s_topd, 16)
            sp.wait_ge(s_topd, 16)
            sp.dma_start(top_i[:, :], dst_top[:].unsqueeze(0).to_broadcast([P, TOP])).then_inc(s_top, 16)
            sp.wait_ge(s_zero, 2)
            sp.dma_start(x_nodes[0:FULL], x[0:FULL * T, :].rearrange("(p t) d -> p t d", p=FULL)).then_inc(s_x, 16)
            if REST:
                sp.dma_start(x_nodes[FULL:FULL + 1, 0:REST], x[FULL * T:N, :].unsqueeze(0)).then_inc(s_x, 16)
            flat_src = src_pad.rearrange("a b -> (a b)")
            sp.dma_start(flat_src[0:E], src[:]).then_inc(s_tab, 16)
            sp.dma_start(flat_src[E:E + SRC_PAD].unsqueeze(0), src_tail[0:1, :]).then_inc(s_tab, 16)

            for h in range(2):
                sp.wait_ge(s_recw[h], 16 * THALF * TITER)
            sp.dma_start(by_rank[:, :, :], records.rearrange("(p t) w -> p t w", p=P)).then_inc(s_rank, 16)

            sp.wait_ge(s_ctl, 3)
            sp.sem_inc(s_rfree, 2)
            with sp.Fori(0, TITER) as it:
                for h in range(2):
                    _, before = tile_counts(sp, it * (2 * THALF) + h * THALF)
                    wait_alone(sp, s_mask, it * (2 * THALF) + (h + 1) * THALF)
                    sp.dma_start(stream[:, bass.ds(before * SLOTS, THALF * RUN)], runs_m[:, h, :]).then_inc(s_wr, 16)
                    wait_alone(sp, s_wr, it * 32 + 16 * (h + 1))
                    sp.sem_inc(s_rfree, 1)
            with sp.If(highest_degree(sp) > RUN):
                with sp.Fori(0, T) as i:
                    n, before = tile_blocks(sp, i)
                    _, chunks_before = tile_counts(sp, i)
                    with sp.Fori(0, n) as b:
                        wait_alone(sp, s_blkm, before + b + 1)
                        col = nc.s_assert_within(chunks_before * SLOTS + b * RUN, 0, STREAM - RUN,
                                                 skip_runtime_bounds_check_because="a tile's blocks start before its end")
                        sp.dma_start(stream[:, bass.ds(col, RUN)], runs_m[:, 0, 0:RUN]).then_inc(s_blkw, 16)
                        wait_alone(sp, s_blkw, (before + b + 1) * 16)
            chunks = total_chunks(sp)
            sp.dma_start(stream[:, bass.ds(chunks * SLOTS, RUN)], zcols[:, :]).then_inc(s_wr, 16)
            sp.wait_ge(s_wr, 16 * (T // THALF + 1))

            def relay_layer(ly):
                for h in range(STAGES):
                    sp.dma_start(stage[:, h, :], stream[:, h * STAGE_COLS:(h + 1) * STAGE_COLS]
                                 ).then_inc(ly.staged[h], 16)
                n = groups(sp)
                with sp.Fori(0, n) as g:
                    for h in range(STAGES):
                        for c in range(STAGE_CHUNKS * h, STAGE_CHUNKS * (h + 1)):
                            sp.wait_ge(ly.got[c], 16 * SLOTS * (g + 1))
                            sp.sem_inc(ly.landed, 1)
                        sp.dma_start(stage[:, h, :], stream[:, bass.ds(g * GROUP_COLS + GROUP_COLS + h * STAGE_COLS, STAGE_COLS)]
                                     ).then_inc(ly.staged[h], 16)
                for h in range(STAGES):
                    wait_alone(sp, ly.staged[h], 16 * (n + 1))

            relay_layer(l0)

            sp.wait_ge(s_row, 16 * (T + 1))
            half = THALF * (WROW + 1)
            for h in range(2):
                sp.dma_start(fin_rows[:, h, :, :].rearrange("p t w -> p (t w)"),
                             ranked_rows[:, h * half:(h + 1) * half]).then_inc(s_fin[h], 16)
            with sp.Fori(0, TITER - 1) as it:
                for h in range(2):
                    sp.wait_ge(s_finw[h], 16 * THALF * (it + 1))
                    sp.dma_start(fin_rows[:, h, :, :].rearrange("p t w -> p (t w)"),
                                 ranked_rows[:, bass.ds(it * (2 * half) + (2 + h) * half, half)]).then_inc(s_fin[h], 16)
            relay_layer(l1)

        @block.vector
        def _(v):
            st = Steps(v, s_dve, wait_alone)

            def bc(t, n):
                return t.unsqueeze(2).to_broadcast([t.shape[0], t.shape[1], n])

            def bc_mid(t, n):
                return t.unsqueeze(1).to_broadcast([t.shape[0], n, t.shape[1]])

            v.memset(ones[:, :], 1.0).then_inc(s_zero, 1)
            st.done(v.memset(zeros[:, :], 0.0))
            st.done(v.memset(one1[:, :], 1.0))
            st.done(v.memset(src_tail[:, :], 0))
            st.done(v.memset(runs_m[:, :, :], ZROW))
            st.done(v.memset(zcols[:, :], ZROW))
            st.done(v.memset(eps_col[:, :], EPS))
            st.done(v.memset(rec[:, :, :], 0))
            st.link(v.memset(x_nodes[96:P], 0.0))
            v.memset(stats[:, :], 0.0).then_inc(s_zero, 1)

            v.wait_ge(s_const, 5)
            st.link(v.tensor_copy(q[:, :], q_i[:, :]))
            v.tensor_scalar(q_mid[:, :], q[:, :], -0.5, None, ALU.add).then_inc(s_q, 1)
            v.wait_ge(s_top, 16)
            v.tensor_copy(top[:, :], top_i[:, :]).then_inc(s_q, 1)
            st.done(v.tensor_copy(iota_bin[:, :], iota_i[:, 0:BINS]))
            st.done(v.tensor_copy(iota_run[:, :], iota_i[:, :]))

            def rows_of(at, after):
                v.wait_ge(s_bal, after)
                st.link(v.tensor_scalar(row[:, at], balance[:, at], 0.5, TOP / 2 - 1, ALU.mult, ALU.add))
                st.link_alone(v.tensor_scalar(row[:, at], row[:, at], 0.0, None, ALU.max))

            def stage_rows(at, a):
                v.tensor_copy(sstage[:, a, :], row[:, at]).then_inc(s_idx, 1)

            def count(it, a):
                v.wait_ge(s_got[a], 16 * PCOLS * (it + 1))
                for k in range(PCOLS):
                    col = bass.ds(it * PASS + a * PCOLS + k, 1)
                    ins = v.tensor_scalar(junk2[:, k, :], got[:, a, k, :], q[:, col], 0.0, ALU.is_lt, ALU.add,
                                          accum_out=below[:, col])
                st.link_alone(ins)

            rows_of(slice(0, PASS), PASS)
            for a in range(PARTS):
                stage_rows(slice(a * PCOLS, (a + 1) * PCOLS), a)
            first, per = st.now(), 2 + PARTS
            with v.Fori(0, SITER - 1) as it:
                st.at(it * per + first)
                rows_of(bass.ds(it * PASS + PASS, PASS), it * PASS + 2 * PASS)
                for a in range(PARTS):
                    count(it, a)
                    stage_rows(bass.ds(it * PASS + PASS + a * PCOLS, PCOLS), a)
                assert st.n == per
            st.at(first + per * (SITER - 1))
            for a in range(PARTS):
                count(SITER - 1, a)
            st.link(v.scalar_tensor_tensor(out=start[:, :], in0=row[:, :], scalar=float(ROW), in1=below[:, :],
                                           op0=ALU.mult, op1=ALU.add))

            st.done(v.tensor_copy(rec[:, :, 0], q_i[:, 0:T]))
            st.done(v.tensor_copy(rec[:, :, 1], start[:, 0:T]))
            st.link(v.tensor_tensor(cols[:, :], start[:, 1:T + 1], start[:, 0:T], ALU.subtract))
            st.done(v.tensor_copy(rec[:, :, 2], cols[:, :]))
            st.link(v.tensor_scalar(bins[:, :], cols[:, :], float(BINS - 1), -1.0, ALU.min, ALU.mult))
            st.link(v.tensor_scalar(bins[:, :], bins[:, :], float(BINS - 1), None, ALU.add))
            st.link(v.tensor_copy(bin_b[:, :], bins[:, :]))
            st.link(v.tensor_tensor(onehot[:, :, :], bc_mid(iota_bin[:, :], T), bc(bins[:, :], BINS), ALU.is_equal))
            st.link(v.tensor_reduce(top_deg[:, :], cols[:, :], AX.X, ALU.max))
            v.tensor_reduce(bin_tot[:, :], onehot[:, :, :].rearrange("p t b -> p b t"), AX.X, ALU.add).then_inc(s_bins, 1)
            v.tensor_tensor(pairs, bc_mid(bin_b[:, :], T), bc(bin_b[:, :], T), ALU.is_equal).then_inc(s_pair, 1)
            v.wait_ge(s_const, 6)
            st.link(v.tensor_reduce(cols2[:, :], pairs, AX.X, ALU.add))
            v.wait_ge(s_binp, 1)
            st.link(v.tensor_copy(bin_tot[:, :], ps_t[:, 0:BINS]))
            st.link(v.tensor_tensor_scan(bin_scan[:, :], ones[:, 0:BINS], bin_tot[:, :], 0.0, ALU.mult, ALU.add))
            st.link(v.tensor_tensor(bin_scan[:, :], bin_scan[:, :], bin_tot[:, :], ALU.subtract))
            st.link(v.tensor_tensor(bin_off[:, :], bin_scan[:, :], ps_u[:, 0:BINS], ALU.add))
            st.link(v.tensor_tensor(onehot[:, :, :], onehot[:, :, :], bc_mid(bin_off[:, :], T), ALU.mult))
            st.link(v.tensor_reduce(cols3[:, :], onehot[:, :, :], AX.X, ALU.add))
            st.link(v.tensor_tensor(cols2[:, :], cols2[:, :], cols3[:, :], ALU.add))
            st.link(v.tensor_copy(icols[:, :], cols2[:, :]))
            st.done(v.tensor_single_scalar(icols2[:, :], icols[:, :], P - 1, ALU.bitwise_and))
            st.link(v.tensor_single_scalar(icols[:, :], icols[:, :], P.bit_length() - 1, ALU.logical_shift_right))
            st.done(v.tensor_copy(cols2[:, :], icols2[:, :]))
            st.link(v.tensor_copy(cols3[:, :], icols[:, :]))
            st.link(v.scalar_tensor_tensor(out=cols[:, :], in0=cols2[:, :], scalar=float(T), in1=cols3[:, :],
                                           op0=ALU.mult, op1=ALU.add))
            st.link(v.tensor_copy(rec[:, :, 4], cols[:, :]))

            def stage_record(tiles_at, h):
                v.tensor_copy(rank_rec[:, h, :, 0:D], x_nodes[:, tiles_at, :]).then_inc(s_rec, 1)
                v.tensor_copy(rank_rec[:, h, :, D:].bitcast(I32), rec[:, tiles_at, :]).then_inc(s_rec, 1)

            v.wait_ge(s_x, X_DMAS)
            for h in range(2):
                stage_record(slice(h * THALF, (h + 1) * THALF), h)
            with v.Fori(0, TITER - 1) as it:
                for h in range(2):
                    wait_alone(v, s_recw[h], 16 * THALF * (it + 1))
                    stage_record(bass.ds(it * (2 * THALF) + (2 + h) * THALF, THALF), h)

            def layer_norm_relu(rows, to, scratch, count):
                st.link(v.tensor_reduce(cols[:, :], rows, AX.X, ALU.add))
                st.link(v.tensor_scalar(cols[:, :], cols[:, :], 1.0 / D, None, ALU.mult))
                st.link(v.tensor_tensor(to, rows, bc(cols[:, :], D), ALU.subtract))
                st.link(v.tensor_tensor(scratch, to, to, ALU.mult))
                v.tensor_reduce(cols2[:, :], scratch, AX.X, ALU.add).then_inc(s_var, 1)
                v.wait_ge(s_std, count)
                st.link(v.reciprocal(cols3[:, :], cols3[:, :]))
                st.link(v.tensor_tensor(to, to, bc(cols3[:, :], D), ALU.mult))
                return v.tensor_scalar(to, to, 0.0, None, ALU.max)

            layer_norm_relu(x_nodes, h_nodes, hr[:, :, :], 1).then_inc(s_h0, 1)

            def stage_tiles(tiles_at, h):
                v.tensor_copy(tstage[:, h, :, :], ranked[:, tiles_at, 0:2]).then_inc(s_tidx, 1)

            v.wait_ge(s_rank, 16)
            for h in range(2):
                stage_tiles(slice(h * THALF, (h + 1) * THALF), h)
            st.link(v.tensor_copy(deg[:, :], ranked[:, :, 2]))
            v.tensor_scalar(rdeg[:, :], deg[:, :], 1.0, None, ALU.max).then_inc(s_degf, 1)
            v.wait_ge(s_degf, 1)
            st.link(v.reciprocal(rdeg[:, :], rdeg[:, :]))
            v.wait_ge(s_degT, 1)
            v.tensor_reduce(cols[0:T, 0:1], ps_y[0:T, 0:P], AX.X, ALU.max).then_inc(s_mxc, 1)
            v.wait_ge(s_mxr, 1)
            st.link(v.tensor_copy(irow[:, 0, :], ps_h[0:1, 0:T]))
            st.link(v.tensor_copy(crow[:, 0, :], ps_h[0:1, 0:T]))
            for at, unit in ((1, SLOTS), (2, RUN)):
                st.link(v.tensor_scalar(crow[:, 3, :], crow[:, 0, :], float(unit - 1), None, ALU.add))
                st.link(v.tensor_copy(irow[:, 3, :], crow[:, 3, :]))
                st.link(v.tensor_single_scalar(irow[:, at, :], irow[:, 3, :], unit.bit_length() - 1,
                                               ALU.logical_shift_right))
                st.link(v.tensor_copy(crow[:, at, :], irow[:, at, :]))
                st.link(v.tensor_scalar(crow[:, at, :], crow[:, at, :], 2.0 if at == 1 else 1.0, None, ALU.max))
                st.link(v.tensor_copy(ctl[:, :, 2 * at - 2], crow[:, at, :]))
                st.link(v.tensor_tensor_scan(crow[:, 3, :], one1[:, :], crow[:, at, :], 0.0, ALU.mult, ALU.add))
                if at == 1:
                    st.link(v.tensor_copy(tot[:, 0:1], crow[:, 3, T - 1:T]))
                    st.link(v.tensor_scalar(cols[0:1, 1:2], crow[:, 3, T - 1:T], float(RING - 1), None, ALU.add))
                    st.link(v.tensor_copy(tot[:, 1:2], cols[0:1, 1:2]))
                    st.link(v.tensor_single_scalar(tot[:, 3:4], tot[:, 1:2], RING.bit_length() - 1,
                                                   ALU.logical_shift_right))
                    st.link(v.tensor_copy(tot[:, 1:2], tot[:, 3:4]))
                    st.link(v.tensor_reduce(crow[:, 2, 0:1], crow[:, 0, :], AX.X, ALU.max))
                    st.link(v.tensor_copy(tot[:, 2:3], crow[:, 2, 0:1]))
                st.link(v.tensor_tensor(crow[:, 3, :], crow[:, 3, :], crow[:, at, :], ALU.subtract))
                v.tensor_copy(ctl[:, :, 2 * at - 1], crow[:, 3, :]).then_inc(s_ctl, 1)
                v.wait_ge(s_ctl, 2 * at - 1)
                if at == 1:
                    halves = crow[:, 3, :].rearrange("p (h t) -> p h t", t=THALF)
                    st.link(v.tensor_tensor(cols_row[:, :].rearrange("p (h t) -> p h t", t=THALF), halves,
                                            halves[:, :, 0:1].to_broadcast([1, T // THALF, THALF]), ALU.subtract))
                    st.link(v.tensor_scalar(cols_row[:, :], cols_row[:, :], float(SLOTS), None, ALU.mult))
                    st.link(v.tensor_tensor(cols_row[:, :], cols_row[:, :], merge_max[:, :], ALU.min))
                    v.tensor_copy(ctl[:, :, 4], cols_row[:, :]).then_inc(s_ctl, 1)

            def mask(got, to, rest, steps, scratch):
                steps.link(v.tensor_tensor(scratch[0], scratch[1], rest, ALU.is_lt))
                steps.link(v.scalar_tensor_tensor(out=scratch[0], in0=got, scalar=float(-ZROW), in1=scratch[0],
                                                  op0=ALU.add, op1=ALU.mult))
                return v.tensor_scalar(to, scratch[0], float(ZROW), None, ALU.add)

            def take_tiles(it, h):
                wait_alone(v, s_land[h], 16 * THALF * (it + 1))
                wait_alone(v, s_rfree, 2 * it + h + 1)
                first_tile = it * (2 * THALF) + h * THALF
                st.link(v.tensor_tensor(valid[:, :, :], bc_mid(iota_run[:, :], THALF),
                                        bc(deg[:, bass.ds(first_tile, THALF)], RUN), ALU.is_lt))
                st.link_alone(v.scalar_tensor_tensor(out=valid[:, :, :], in0=runs[:, h, :, :], scalar=float(-ZROW),
                                                     in1=valid[:, :, :], op0=ALU.add, op1=ALU.mult))
                for k in range(THALF):
                    at = v.value_load(ctl[0:1, bass.ds(first_tile + k, 1), 4:5].rearrange("p a b -> p (a b)"),
                                      min_val=0, max_val=(THALF - 1) * RUN)
                    v.tensor_scalar(runs_m[:, h, bass.ds(at, RUN)], valid[:, k, :], float(ZROW), None,
                                    ALU.add).then_inc(s_mask, 1)
                    wait_alone(v, s_mask, first_tile + k + 1)

            first, per = st.now(), 2 * 2
            with v.Fori(0, TITER - 1) as it:
                st.at(it * per + first)
                for h in range(2):
                    take_tiles(it, h)
                    stage_tiles(bass.ds(it * (2 * THALF) + (2 + h) * THALF, THALF), h)
                assert st.n == per
            st.at(first + per * (TITER - 1))
            for h in range(2):
                take_tiles(TITER - 1, h)

            gen = Steps(v, s_gen, wait_alone)
            offset, left = cols2[:, 0:1], cols2[:, 1:2]
            with v.If(highest_degree(v) > RUN):
                with v.Fori(0, T) as i:
                    n, before = tile_blocks(v, i)
                    gen.at((before * 4) + (i * 2))
                    gen.done(v.tensor_copy(offset, at_tile(ranked, i, 1, 2)))
                    gen.link_alone(v.tensor_copy(left, at_tile(ranked, i, 2, 3)))
                    with v.Fori(0, n) as b:
                        gen.at((before + b) * 4 + (i * 2 + 2))
                        v.tensor_scalar(tstage[:, 0, 0, 1:2], offset, float(E), None, ALU.min).then_inc(s_blk, 1)
                        v.wait_ge(s_blkl, (before + b + 1) * 16)
                        v.wait_ge(s_blk, before + b + 1)
                        mask(runs[:, 0, 0, :], runs_m[:, 0, 0:RUN], left.to_broadcast([P, RUN]), gen,
                             (valid[:, 0, :], iota_run[:, :])).then_inc(s_blkm, 1)
                        gen.done(v.tensor_scalar(offset, offset, float(RUN), None, ALU.add))
                        gen.link(v.tensor_scalar(left, left, float(-RUN), None, ALU.add))
                        wait_alone(v, s_blkm, before + b + 1)
                        wait_alone(v, s_blkw, (before + b + 1) * 16)
                        v.nop()

            v.wait_ge(s_h0w, 32)
            layer_norm_relu(xr, hr[:, :, :], x_nodes, 2).then_inc(s_hr, 1)
            v.wait_ge(s_hr, 1)

            first, per = st.now(), 6
            with v.Fori(0, T) as i:
                st.at(i * per + first)
                v.wait_ge(l0.sum, i + 1)
                v.tensor_scalar(cat[:, D:2 * D], ps_sum[:, 0:D], rdeg[:, bass.ds(i, 1)], None,
                                ALU.mult).then_inc(l0.cat, 1)
                v.tensor_copy(cat[:, 0:D], at_tile(hr, i)).then_inc(l0.cat, 1)
                v.wait_ge(l0.y, i + 1)
                st.link_alone(v.scalar_tensor_tensor(out=at_tile(xr, i), in0=ps_y[:, 0:D], scalar=0.0,
                                                     in1=at_tile(xr, i), op0=ALU.max, op1=ALU.add))
                st.link_alone(v.bn_stats(stats[:, :], at_tile(xr, i)))
                v.bn_aggr(mv[:, :], stats[:, :]).then_inc(s_var1, 1)
                v.wait_ge(s_std1, i + 1)
                st.link(v.reciprocal(rstd[:, :], std[:, :]))
                v.wait_ge(s_row, 16 * (i + 1))
                st.link(v.tensor_scalar(rowbuf[:, 0:D], at_tile(xr, i), mv[:, 0:1], rstd[:, 0:1],
                                        ALU.subtract, ALU.mult))
                v.tensor_scalar(rowbuf[:, 0:D], rowbuf[:, 0:D], 0.0, None, ALU.max).then_inc(s_h1, 1)
                wait_alone(v, s_h1, i + 1)
                st.done(v.tensor_copy(at_tile(hr, i), rowbuf[:, 0:D]))
                st.link_alone(v.tensor_copy(rowbuf[:, WROW:WROW + 1].bitcast(I32), at_tile(ranked, i, 0, 1)))
                wait_alone(v, s_ab, i + 1)
                v.tensor_copy(at_tile(b_self, i), ps_h[:, 0:H]).then_inc(l0.tile, 1)
                assert st.n == per
            st.at(first + per * T)

            v.wait_ge(l0.tile, T)
            v.wait_ge(s_ctl, 3)
            first = st.now()

            def pre_act(w, i):
                v.wait_ge(l1.landed, w + 1)
                rows = ring1[:, bass.ds(w & (RING - 1), 1), :, :].rearrange("p c s w -> p (c s) w")
                v.tensor_tensor(pre[:, :, :], rows[:, :, D:WROW],
                                b_self[:, bass.ds(i, 1), :].to_broadcast([P, SLOTS, H]), ALU.add).then_inc(s_pre, 1)

            def weigh(w):
                v.wait_ge(s_pre, w + 1)
                v.scalar_tensor_tensor(out=act_w[:, :, :], in0=pre[:, :, :], scalar=0.0,
                                       in1=bc_mid(we2_rows[:, :], SLOTS), op0=ALU.max, op1=ALU.mult).then_inc(s_act, 1)

            def score(w):
                v.wait_ge(s_act, w + 1)
                v.tensor_reduce(z[:, :], act_w[:, :, :], AX.X, ALU.add).then_inc(s_z, 1)

            def message(w):
                v.wait_ge(s_gate, w + 1)
                v.wait_ge(s_msgf, w + 1)
                rows = ring1[:, bass.ds(w & (RING - 1), 1), :, :].rearrange("p c s w -> p (c s) w")
                v.tensor_tensor(msg[:, :, :], rows[:, :, 0:D], bc(gate[:, :], D), ALU.mult).then_inc(s_msg, 1)

            def chunk_maximum(w):
                v.wait_ge(s_msg, w + 1)
                v.wait_ge(s_acc, w + 1)
                v.tensor_reduce(chunk_max[:, :], msg[:, :, :].rearrange("p s d -> p d s"), AX.X,
                                ALU.max).then_inc(l1.used, 1)

            def maximum(w):
                v.wait_ge(l1.used, w + (RING + 1))
                v.tensor_tensor(cat[:, 0:D], cat[:, 0:D], chunk_max[:, :], ALU.max).then_inc(s_acc, 1)

            def finish(i):
                v.wait_ge(l1.y, i + 1)
                st.link(v.tensor_tensor(rowbuf[:, 0:D], ps_y[:, 0:D], at_tile(hr, i), ALU.add))
                st.done(v.tensor_tensor(at_tile(xr, i), rowbuf[:, 0:D], at_tile(xr, i), ALU.add))

            def tile(i, before_it):
                n, before = tile_counts(v, i)
                if before_it is not None:
                    wait_alone(v, l1.catT, i)
                st.link_alone(v.memset(cat[:, 0:D], 0.0))
                w = v.snap(before + 0)
                pre_act(w, i)
                weigh(w)
                score(w)
                if before_it is not None:
                    finish(before_it)
                with v.Fori(1, n) as c:
                    w = v.snap(before + c)
                    last = v.snap(w - 1)
                    pre_act(w, i)
                    message(last)
                    weigh(w)
                    chunk_maximum(last)
                    score(w)
                    maximum(last)
                last = v.snap(before + n - 1)
                message(last)
                chunk_maximum(last)
                maximum(last)
                wait_alone(v, l1.sum, i + 1)
                v.tensor_copy(h_tile[:, :], at_tile(hr, i)).then_inc(l1.cat, 1)
                v.tensor_copy(cat[:, D:2 * D], ps_sum[:, 0:D]).then_inc(l1.cat, 1)

            v.sem_inc(s_acc, 1)
            tile(0, None)
            first, per = st.now(), 3
            with v.Fori(1, T) as i:
                st.at(i * per + (first - per))
                tile(i, i - 1)
                assert st.n == per
            st.at(first + per * (T - 1))
            finish(T - 1)
            st.wait()


            def stage_out(tiles_at, h):
                v.tensor_copy(out_rows[:, h, :, :], xr[:, tiles_at, :]).then_inc(s_outs, 1)
                v.tensor_copy(out_idx[:, h, :, :], ranked[:, tiles_at, 0:2]).then_inc(s_outs, 1)

            for h in range(2):
                stage_out(slice(h * THALF, (h + 1) * THALF), h)
            with v.Fori(0, TITER - 1) as it:
                for h in range(2):
                    wait_alone(v, s_outw[h], 16 * THALF * (it + 1))
                    stage_out(bass.ds(it * (2 * THALF) + (2 + h) * THALF, THALF), h)

        @block.scalar
        def _(act):
            def load(to, frm):
                act.dma_start(to, frm).then_inc(s_w, 16)

            act.wait_ge(s_q, 2)
            with act.Fori(0, SITER) as it:
                for k in range(PASS):
                    col = bass.ds(it * PASS + k, 1)
                    act.activation(junk[:, k, :], top[:, :], ACT.Sign, scale=-1.0, bias=q_mid[:, col],
                                   accum_out=balance[:, col]).then_inc(s_bal, 1)
                wait_alone(act, s_bal, it * PASS + PASS)

            load(w_cat[0:D, :], w_self[:, :])
            load(w_cat[D:2 * D, :], w_neigh[:, :])
            load(w_ab[:, 0:H], we1[0:D, :])
            load(w_ab[:, H:2 * H], we1[D:2 * D, :])
            load(w_n1a[:, :], wn1[0:2 * D, :])
            load(w_n1b[:, :], wn1[2 * D:3 * D, :])
            load(w_n2[:, :], wn2[:, :])
            load(b0_row[:, :], b0[:].unsqueeze(0))
            load(bn2_row[:, :], bn2[:].unsqueeze(0))
            load(bn1_col[:, :], bn1[:].unsqueeze(1))
            load(be2_col[:, :], be2[:].unsqueeze(0).to_broadcast([P, 1]))
            load(we2_rows[:, :], we2.rearrange("h a -> a h").to_broadcast([P, H]))
            load(be1_row[:, :], be1[:].unsqueeze(0))
            act.dma_start(h0_table[ZROW:ZROW + 1, :], zeros[0:1, 0:D]).then_inc(s_h0w, 16)
            act.dma_start(hA_table[ZROW:ZROW + 1, :], zeros[0:1, :]).then_inc(s_row, 16)

            act.wait_ge(s_var, 1)
            act.activation(cols3[:, :], cols2[:, :], ACT.Sqrt, bias=eps_col[:, 0:1], scale=1.0 / D).then_inc(s_std, 1)
            act.wait_ge(s_h0, 1)
            act.dma_start(h0_table[0:NP, :].rearrange("(p t) d -> p t d", p=P), h_nodes).then_inc(s_h0w, 16)
            act.wait_ge(s_var, 2)
            act.activation(cols3[:, :], cols2[:, :], ACT.Sqrt, bias=eps_col[:, 0:1], scale=1.0 / D).then_inc(s_std, 1)

            act.wait_ge(s_w, W_DMAS)
            with act.Fori(0, T) as i:
                act.wait_ge(l0.catT, i + 1)
                act.activation(catT[:, :], ps_t[:, 0:P], ACT.Copy).then_inc(l0.catTs, 1)
                act.wait_ge(s_var1, i + 1)
                act.activation(std[:, :], mv[:, 1:2], ACT.Sqrt, bias=eps_col[:, 0:1]).then_inc(s_std1, 1)
                act.wait_ge(s_h1T, i + 1)
                act.activation(hT[:, :], ps_u[0:D, 0:P], ACT.Copy).then_inc(s_h1Ts, 1)
                act.wait_ge(s_ab, i + 1)
                act.activation(rowbuf[:, D:WROW], ps_a[:, 0:H], ACT.Copy).then_inc(s_rowA, 1)
                act.wait_ge(s_rowA, i + 1)
                act.wait_ge(l0.tile, i + 1)
                act.dma_start(ranked_rows[:, bass.ds(i * (WROW + 1), WROW + 1)], rowbuf[:, :]).then_inc(s_row, 16)

            with act.Fori(0, T) as i:
                n, before = tile_counts(act, i)
                with act.Fori(0, n) as c:
                    w = act.snap(before + c)
                    act.wait_ge(s_z, w + 1)
                    act.activation(gate[:, :], z[:, :], ACT.Sigmoid, bias=be2_col[:, 0:1]).then_inc(s_gate, 1)
                act.wait_ge(l1.catT, i + 1)
                act.activation(catT[:, :], ps_t[:, 0:P], ACT.Copy).then_inc(l1.catTs, 1)
                act.activation(hT[:, :], ps_u[0:D, 0:P], ACT.Copy).then_inc(l1.catTs, 1)
                act.wait_ge(s_hid, i + 1)
                act.activation(h2T[:, :], ps_h[:, 0:P], ACT.Relu, bias=bn1_col[:, 0:1]).then_inc(s_hids, 1)

        @block.tensor
        def _(pe):
            pe.wait_ge(s_const, 5)
            pe.wait_ge(s_bins, 1)
            pe.matmul(ps_t[:, 0:BINS], ones[:, :], bin_tot[:, :], start=True, stop=True)
            pe.matmul(ps_u[:, 0:BINS], upper[:, :], bin_tot[:, :], start=True, stop=True).then_inc(s_binp, 1)
            pe.wait_ge(s_degf, 1)
            pe.transpose(ps_y[0:T, 0:P], deg[:, :], ident[:, :]).then_inc(s_degT, 1)
            pe.wait_ge(s_mxc, 1)
            pe.transpose(ps_h[0:1, 0:T], cols[0:T, 0:1], ident[0:T, 0:T]).then_inc(s_mxr, 1)
            pe.wait_ge(s_ctl, 3)
            pe.wait_ge(s_w, W_DMAS)

            def sum_start():
                pe.matmul(ps_sum[:, 0:D], zeros[0:1, 0:P], zeros[0:1, 0:D], start=True, stop=False,
                          skip_group_check=True)

            def sum_add(rows):
                return pe.matmul(ps_sum[:, 0:D], ident[:, :], rows, start=False, stop=False, skip_group_check=True)

            def sum_stop():
                return pe.matmul(ps_sum[:, 0:D], zeros[0:1, 0:P], zeros[0:1, 0:D], start=False, stop=True,
                                 skip_group_check=True)

            pe.sem_inc(l0.used, RING)
            with pe.Fori(0, T) as i:
                n, before = tile_counts(pe, i)
                sum_start()
                with pe.Fori(0, n) as c:
                    w = pe.snap(before + c)
                    place = pe.snap(w & (RING - 1))
                    pe.wait_ge(l0.landed, w + 1)
                    for s in range(SLOTS):
                        last = sum_add(ring0[:, bass.ds(place, 1), s, :].rearrange("p c w -> p (c w)"))
                    last.then_inc(l0.used, 1)
                sum_stop().then_inc(l0.sum, 1)
                pe.wait_ge(l0.cat, 2 * i + 2)
                pe.transpose(ps_t[:, 0:P], cat[:, :], ident[:, :]).then_inc(l0.catT, 1)
                pe.wait_ge(l0.catTs, i + 1)
                pe.matmul(ps_y[:, 0:D], catT[:, :], w_cat[:, :], start=True, stop=False)
                pe.matmul(ps_y[:, 0:D], ones[0:1, 0:P], b0_row[:, :], start=False, stop=True).then_inc(l0.y, 1)
                wait_alone(pe, s_h1, i + 1)
                pe.transpose(ps_u[0:D, 0:P], rowbuf[:, 0:D], ident[:, :]).then_inc(s_h1T, 1)
                pe.wait_ge(s_h1Ts, i + 1)
                pe.matmul(ps_a[:, 0:H], hT[:, :], w_ab[:, 0:H], start=True, stop=True)
                pe.matmul(ps_h[:, 0:H], hT[:, :], w_ab[:, H:2 * H], start=True, stop=False)
                pe.matmul(ps_h[:, 0:H], ones[0:1, 0:P], be1_row[:, :], start=False, stop=True).then_inc(s_ab, 1)

            pe.sem_inc(l1.used, RING)
            pe.sem_inc(s_msgf, 1)
            with pe.Fori(0, T) as i:
                n, before = tile_counts(pe, i)
                sum_start()
                with pe.Fori(0, n) as c:
                    w = pe.snap(before + c)
                    pe.wait_ge(s_msg, w + 1)
                    for s in range(SLOTS):
                        last = sum_add(msg[:, s, :])
                    last.then_inc(s_msgf, 1)
                sum_stop().then_inc(l1.sum, 1)
                wait_alone(pe, l1.cat, 2 * i + 2)
                pe.transpose(ps_u[0:D, 0:P], h_tile[:, :], ident[:, :])
                pe.transpose(ps_t[:, 0:P], cat[:, :], ident[:, :]).then_inc(l1.catT, 1)
                pe.wait_ge(l1.catTs, 2 * i + 2)
                pe.matmul(ps_h[:, 0:P], w_n1a[:, :], catT[:, :], start=True, stop=False)
                pe.matmul(ps_h[:, 0:P], w_n1b[:, :], hT[:, :], start=False, stop=True).then_inc(s_hid, 1)
                pe.wait_ge(s_hids, i + 1)
                pe.matmul(ps_y[:, 0:D], h2T[:, :], w_n2[:, :], start=True, stop=False)
                pe.matmul(ps_y[:, 0:D], ones[0:1, 0:P], bn2_row[:, :], start=False, stop=True).then_inc(l1.y, 1)


_INS = ['x', 'src', 'dst', 'L0_gnn_W_self', 'L0_gnn_W_neigh', 'L0_gnn_b', 'L1_gnn_We1', 'L1_gnn_be1', 'L1_gnn_We2',
        'L1_gnn_be2', 'L1_gnn_Wn1', 'L1_gnn_bn1', 'L1_gnn_Wn2', 'L1_gnn_bn2']


def kernel(**inputs):
    import numpy as _np
    import concourse.bacc as _bacc
    from concourse import mybir as _mybir
    from concourse.bass_utils import run_bass_kernel_spmd as _run

    nc = _bacc.Bacc("TRN2", target_bir_lowering=False, num_devices=1)
    arrays, args = {}, []
    for name in _INS:
        a = _np.ascontiguousarray(inputs[name])
        arrays[f"in_{name}_dram"] = a
        args.append(nc.dram_tensor(f"in_{name}_dram", a.shape, _mybir.dt.from_np(a.dtype), kind="ExternalInput").ap())
    args.append(nc.dram_tensor("out_dram", inputs['x'].shape, _mybir.dt.float32, kind="ExternalOutput").ap())
    gnn_kernel(nc, *args)
    r = _run(nc, [arrays], core_ids=[0])
    return r.results[0]["out_dram"]
```

```python
from contextlib import ExitStack

import concourse.bass as bass
from concourse import mybir

F32 = mybir.dt.float32
BF16 = mybir.dt.bfloat16
I32 = mybir.dt.int32
ALU = mybir.AluOpType
ACT = mybir.ActivationFunctionType
AX = mybir.AxisListType

P = 128
EPS = 1e-5

SLOTS = 4
STAGES = 2
STAGE_COLS = 16
GROUP_COLS = STAGES * STAGE_COLS
PLACES = GROUP_COLS // SLOTS
STAGE_CHUNKS = STAGE_COLS // SLOTS

RUN = 64
BINS = 64
PARTS = 5
PCOLS = 2
REC = 4


class Steps:

    def __init__(self, eng, sem, alone):
        self.eng, self.sem, self.alone, self.base, self.n = eng, sem, alone, 0, 0

    def done(self, ins):
        ins.then_inc(self.sem, 1)
        self.n += 1

    def wait(self):
        self.eng.wait_ge(self.sem, self.base + self.n)

    def link(self, ins):
        self.done(ins)
        self.wait()

    def link_alone(self, ins):
        self.done(ins)
        self.alone(self.eng, self.sem, self.base + self.n)

    def at(self, base):
        self.base, self.n = base, 0

    def now(self):
        return self.base + self.n


def gnn_kernel(nc, x, src, dst, w_self, w_neigh, b0, we1, be1, we2, be2, wn1, bn1, wn2, bn2, out):
    N, D = x.shape
    E = src.shape[0]
    H = we1.shape[1]
    T = -(-N // P)
    NP = T * P
    ZROW = NP
    NROWS = NP + 1
    FULL = N // T
    REST = N - FULL * T

    ROW = max(r for r in range(1, T * D // (PARTS * PCOLS) + 1) if E % r == 0)
    TOP = E // ROW
    PASS = PARTS * PCOLS
    SITER = -(-(T + 1) // PASS)
    SCOLS = SITER * PASS
    THALF = 7
    TITER = T // (2 * THALF)
    FIRST = 4 * THALF
    assert TITER * 2 * THALF == T and T <= P and THALF * (SLOTS + 1) >= GROUP_COLS

    SRC_ROWS = -(-(E + RUN) // RUN)
    SRC_PAD = SRC_ROWS * RUN - E
    MAXCOLS = E + T * (SLOTS + 1)
    MAXCHUNKS = MAXCOLS // SLOTS + T
    MAXBLOCKS = E // RUN + T + 1
    STREAM = (MAXCOLS // RUN + 3 + THALF) * RUN

    def dram(name, shape, dt):
        return nc.dram_tensor(name, shape, dt).ap()

    dst_rows = dst.rearrange("(a b) -> a b", b=ROW)
    dst_top = dram("dst_top", (TOP,), I32)
    src_pad = dram("src_pad", (SRC_ROWS, RUN), I32)
    h0_table = dram("h0_table", (NROWS, D), F32)
    records = dram("records", (NP, D + REC), F32)
    stream = dram("stream", (P, STREAM), I32)
    WROW = D + H
    ranked_rows = dram("ranked_rows", (P, T * (WROW + 1)), F32)
    hA_table = dram("hA_table", (NROWS, WROW), F32)

    with ExitStack() as ctx:
        def sb(name, shape, dt=F32):
            return ctx.enter_context(nc.sbuf_tensor(name, shape, dt))

        def psum(name, shape):
            return ctx.enter_context(nc.psum_tensor(name, shape, F32))

        def sem(name):
            return ctx.enter_context(nc.semaphore(name))

        ident = sb("ident", [P, P])
        upper = sb("upper", [P, P])
        ones = sb("ones", [P, P])
        w_cat = sb("w_cat", [2 * D, D])
        w_ab = sb("w_ab", [D, 2 * H])
        w_n1a = sb("w_n1a", [2 * D, H])
        w_n1b = sb("w_n1b", [D, H])
        w_n2 = sb("w_n2", [H, D])
        b0_row = sb("b0_row", [1, D])
        be1_row = sb("be1_row", [1, H])
        bn2_row = sb("bn2_row", [1, D])
        bn1_col = sb("bn1_col", [H, 1])
        be2_col = sb("be2_col", [P, 1])
        eps_col = sb("eps_col", [P, 1])
        we2_rows = sb("we2_rows", [P, H])
        src_tail = sb("src_tail", [1, SRC_PAD], I32)
        zeros = sb("zeros", [P, WROW])
        zcols = sb("zcols", [P, RUN], I32)

        rec = sb("rec", [P, T, REC + 1], I32)
        by_rank = sb("by_rank", [P, T, D + REC])
        xr = by_rank[:, :, 0:D]
        ranked = by_rank[:, :, :].bitcast(I32)[:, :, D:D + REC]
        deg = sb("deg", [P, T])
        rdeg = sb("rdeg", [P, T])
        ctl = sb("ctl", [1, T, 8], I32)
        tot = sb("tot", [1, 4], I32)
        hr = sb("hr", [P, T, D])
        b_self = sb("b_self", [P, T, H])
        ring = sb("ring", [P, (GROUP_COLS + SLOTS - 1) * WROW])
        stage = sb("stage", [P, STAGES, STAGE_COLS], I32)

        x_nodes = b_self[:, :, 0:D]
        h_nodes = b_self[:, :, D:2 * D]
        onehot_flat = hr[:, :, :].rearrange("p t d -> p (t d)")[:, 0:BINS * T]
        order_flat = by_rank[:, :, :].rearrange("p t d -> p (t d)")[:, 0:BINS * T]
        onehot = onehot_flat.rearrange("p (b t) -> p b t", b=BINS)
        order = order_flat.rearrange("p (b t) -> p b t", b=BINS)

        q = sb("q", [P, SCOLS])
        q_mid = sb("q_mid", [P, SCOLS])
        top = sb("top", [P, TOP])
        top_i = sb("top_i", [P, TOP], I32)
        signs = sb("signs", [P, PASS, TOP], BF16)
        below_out = sb("below_out", [P, PCOLS, ROW], BF16)
        balance = sb("balance", [P, SCOLS])
        row = sb("row", [P, SCOLS])
        below = sb("below", [P, SCOLS])
        start = sb("start", [P, SCOLS])
        sstage = sb("sstage", [P, PARTS, PCOLS], I32)
        cols = sb("cols", [P, T])
        cols2 = sb("cols2", [P, T])
        cols3 = sb("cols3", [P, T])
        icols = sb("icols", [P, T], I32)
        icols2 = sb("icols2", [P, T], I32)
        top_deg = sb("top_deg", [P, 1])
        tile_i = sb("tile_i", [P, 1], I32)
        tile_rank = sb("tile_rank", [P, 1])
        classes = sb("classes", [P, 1])
        over = sb("over", [1, 1])
        bins = sb("bins", [P, T])
        bin_before = sb("bin_before", [P, BINS])
        iota_bin = sb("iota_bin", [P, BINS])
        iota_run = sb("iota_run", [P, RUN])
        iota_i = sb("iota_i", [P, RUN], I32)
        q_i = sb("q_i", [P, SCOLS], I32)
        bin_tot = sb("bin_tot", [P, BINS])
        bin_scan = sb("bin_scan", [P, BINS])
        bin_off = sb("bin_off", [P, BINS])
        rank_rec = sb("rank_rec", [P, 2, THALF, D + REC + 1])
        tstage = sb("tstage", [P, 2, THALF, 2], I32)
        out_rows = sb("out_rows", [P, 2, THALF, D])
        runs = sb("runs", [P, 2, THALF, RUN], I32)
        runs_m = sb("runs_m", [P, 2, THALF * RUN], I32)
        merge_max = sb("merge_max", [1, T], I32)
        valid = sb("valid", [P, THALF, RUN])
        crow = sb("crow", [1, 4, T])
        irow = sb("irow", [1, 2, T], I32)
        one1 = sb("one1", [1, T])

        cat = sb("cat", [P, 2 * D])
        catT = sb("catT", [P, P])
        hT = sb("hT", [D, P])
        h_tile = sb("h_tile", [P, D])
        h2T = sb("h2T", [H, P])
        rowbuf = sb("rowbuf", [P, WROW + 1])
        stats = sb("stats", [P, 6])
        mv = sb("mv", [P, 2])
        std = sb("std", [P, 1])
        rstd = sb("rstd", [P, 1])
        pre = sb("pre", [P, SLOTS, H])
        act_w = sb("act_w", [P, SLOTS, H])
        z = sb("z", [P, SLOTS])
        gate = sb("gate", [P, SLOTS])
        msg = sb("msg", [P, SLOTS, D])
        chunk_max = sb("chunk_max", [P, D])

        got = hr[:, :, :].rearrange("p t d -> p (t d)")[:, 0:PASS * ROW].bitcast(I32).rearrange(
            "p (a b r) -> p a b r", a=PARTS, b=PCOLS)
        fin_rows = ring[:, GROUP_COLS * D:GROUP_COLS * D + 2 * THALF * (WROW + 1)].rearrange(
            "p (h t w) -> p h t w", h=2, t=THALF)
        ring0 = ring[:, 0:GROUP_COLS * D].rearrange("p (s w) -> p s w", w=D)
        ring1 = ring[:, :].rearrange("p (s w) -> p s w", w=WROW)
        out_idx = tstage

        ps_sum = psum("ps_sum", [P, 512])
        ps_t = psum("ps_t", [P, 512])
        ps_u = psum("ps_u", [P, 512])
        ps_y = psum("ps_y", [P, 512])
        ps_a = psum("ps_a", [P, 512])
        ps_h = psum("ps_h", [P, 512])

        s_passed = sem("s_passed")
        s_const = sem("s_const")
        s_zero = sem("s_zero")
        s_topd = sem("s_topd")
        s_top = sem("s_top")
        s_w = sem("s_w")
        s_x = sem("s_x")
        s_tab = sem("s_tab")
        s_dve = sem("s_dve")
        s_q = sem("s_q")
        s_bal = sem("s_bal")
        s_idx = sem("s_idx")
        s_got = [sem(f"s_got{a}") for a in range(PARTS)]
        s_bins = sem("s_bins")
        s_binp = sem("s_binp")
        s_gen = sem("s_gen")
        s_rfree = sem("s_rfree")
        s_rec = sem("s_rec")
        s_recw = [sem(f"s_recw{h}") for h in range(2)]
        s_rank = [sem(f"s_rank{k}") for k in range(2)]
        s_var = sem("s_var")
        s_std = sem("s_std")
        s_h0 = sem("s_h0")
        s_h0w = sem("s_h0w")
        s_degf = sem("s_degf")
        s_mxr = sem("s_mxr")
        s_ctl = sem("s_ctl")
        s_tidx = sem("s_tidx")
        s_land = [sem(f"s_land{h}") for h in range(2)]
        s_mask = sem("s_mask")
        s_wr = sem("s_wr")
        s_blk = sem("s_blk")
        s_blkl = sem("s_blkl")
        s_blkm = sem("s_blkm")
        s_blkw = sem("s_blkw")

        class Layer:
            def __init__(self, n):
                self.staged = [sem(f"s_staged{n}_{h}") for h in range(STAGES)]
                self.got = [sem(f"s_got{n}_{c}") for c in range(PLACES)]
                self.landed = sem(f"s_landed{n}")
                self.used = sem(f"s_used{n}")
                self.sum = sem(f"s_sum{n}")
                self.cat = sem(f"s_cat{n}")
                self.catT = sem(f"s_catT{n}")
                self.catTs = sem(f"s_catTs{n}")
                self.y = sem(f"s_y{n}")
                self.tile = sem(f"s_tile{n}")

        l0, l1 = Layer(0), Layer(1)
        s_var1 = sem("s_var1")
        s_std1 = sem("s_std1")
        s_h1 = sem("s_h1")
        s_h1T = sem("s_h1T")
        s_h1Ts = sem("s_h1Ts")
        s_ab = sem("s_ab")
        s_rowA = sem("s_rowA")
        s_row = sem("s_row")
        s_fin = [sem(f"s_fin{h}") for h in range(2)]
        s_finw = [sem(f"s_finw{h}") for h in range(2)]
        s_pre = sem("s_pre")
        s_act = sem("s_act")
        s_mirror = sem("s_mirror")
        s_cmax = sem("s_cmax")
        s_acc = sem("s_acc")
        s_z = sem("s_z")
        s_gate = sem("s_gate")
        s_msg = sem("s_msg")
        s_msgf = sem("s_msgf")
        s_hid = sem("s_hid")
        s_hids = sem("s_hids")
        s_outs = sem("s_outs")
        s_outw = [sem(f"s_outw{h}") for h in range(2)]

        def tile_word(eng, i, at, low, high):
            return eng.value_load(ctl[0:1, bass.ds(i, 1), at:at + 1].rearrange("p a b -> p (a b)"),
                                  min_val=low, max_val=high)

        def tile_slots(eng, i):
            return tile_word(eng, i, 0, SLOTS + 1, MAXCOLS), tile_word(eng, i, 1, 0, MAXCOLS)

        def tile_chunks(eng, i):
            return tile_word(eng, i, 5, 2, MAXCHUNKS), tile_word(eng, i, 6, 0, MAXCHUNKS)

        def tile_blocks(eng, i):
            return tile_word(eng, i, 2, 1, MAXBLOCKS), tile_word(eng, i, 3, 0, MAXBLOCKS)

        def groups(eng):
            return eng.value_load(tot[0:1, 1:2], min_val=1, max_val=MAXCOLS // GROUP_COLS + 1)

        def highest_degree(eng):
            return eng.value_load(tot[0:1, 2:3], min_val=0, max_val=E)

        def at_tile(t, i, lo=0, hi=None):
            hi = t.shape[2] if hi is None else hi
            return t[:, bass.ds(i, 1), lo:hi].rearrange("p a b -> p (a b)")

        def wait_alone(eng, s, value):
            eng.wait_ge(s, value)
            eng.sem_inc(s_passed, 1)

        TAB_DMAS = 16 * 2
        X_DMAS = 16 * (2 if REST else 1)
        W_DMAS = 16 * 13
        H0_DMAS = 16 * (1 + 2 * TITER)

        block = ctx.enter_context(nc.Block())

        @block.gpsimd
        def _(pool):
            pool.iota(q_i[:, :], pattern=[[1, SCOLS]], base=0, channel_multiplier=T).then_inc(s_const, 1)
            pool.iota(iota_i[:, :], pattern=[[1, RUN]], base=0, channel_multiplier=0).then_inc(s_const, 1)
            pool.iota(tile_i[:, :], pattern=[[0, 1]], base=1, channel_multiplier=P).then_inc(s_const, 1)
            pool.wait_ge(s_zero, 1)
            pool.affine_select(out=ident[:, :], in_=ones[:, :], compare_op=ALU.is_equal, fill=0.0, base=0,
                               pattern=[[-1, P]], channel_multiplier=1).then_inc(s_const, 1)
            pool.iota(merge_max[:, :], pattern=[[0, T // THALF], [RUN, THALF]], base=0,
                      channel_multiplier=0).then_inc(s_const, 1)
            pool.affine_select(out=upper[:, :], in_=ones[:, :], compare_op=ALU.is_gt, fill=0.0, base=0,
                               pattern=[[1, P]], channel_multiplier=-1).then_inc(s_const, 1)

            def gather(to, table, idx, axis=0):
                return pool.indirect_dma_start(to, None, table, bass.IndirectOffsetOnAxis(ap=idx, axis=axis))

            with pool.Fori(0, SITER) as it:
                for a in range(PARTS):
                    wait_alone(pool, s_idx, it * PARTS + a + 1)
                    for k in range(PCOLS):
                        gather(got[:, a, k, :], dst_rows, sstage[:, a, k:k + 1]).then_inc(s_got[a], 16)

            with pool.Fori(0, TITER) as it:
                for h in range(2):
                    wait_alone(pool, s_rec, 4 * it + 2 * h + 2)
                    for k in range(THALF):
                        pool.indirect_dma_start(
                            records[:, :], bass.IndirectOffsetOnAxis(
                                ap=rank_rec[:, h, k, D + REC:D + REC + 1].bitcast(I32), axis=0),
                            rank_rec[:, h, k, 0:D + REC], None).then_inc(s_recw[h], 16)

            pool.wait_ge(s_tab, TAB_DMAS)
            with pool.Fori(0, TITER) as it:
                for h in range(2):
                    wait_alone(pool, s_tidx, 2 * it + h + 1)
                    for k in range(THALF):
                        gather(runs[:, h, k, :], src_pad[:, :], tstage[:, h, k, 1:2], axis=1).then_inc(s_land[h], 16)

            pool.wait_ge(s_ctl, 4)
            with pool.If(highest_degree(pool) > RUN):
                with pool.Fori(0, T) as i:
                    n, before = tile_blocks(pool, i)
                    with pool.Fori(0, n) as b:
                        wait_alone(pool, s_blk, before + b + 1)
                        gather(runs[:, 0, 0, :], src_pad[:, :], tstage[:, 0, 0, 1:2], axis=1).then_inc(s_blkl, 16)

            def gather_layer(ly, table, places, ready, ready_at):
                pool.wait_ge(ready, ready_at)
                with pool.Fori(0, groups(pool)) as g:
                    for h in range(STAGES):
                        wait_alone(pool, ly.staged[h], 16 * (g + 1))
                        for c in range(STAGE_CHUNKS * h, STAGE_CHUNKS * (h + 1)):
                            wait_alone(pool, ly.used, g * GROUP_COLS + (c + 1) * SLOTS)
                            for s in range(SLOTS):
                                col = (c * SLOTS + s) % STAGE_COLS
                                gather(places[:, c * SLOTS + s, :], table[:, :],
                                       stage[:, h, col:col + 1]).then_inc(ly.got[c], 16)

            gather_layer(l0, h0_table, ring0, s_h0w, H0_DMAS)

            with pool.Fori(0, TITER) as it:
                for h in range(2):
                    wait_alone(pool, s_fin[h], 16 * (it + 1))
                    for k in range(THALF):
                        pool.indirect_dma_start(
                            hA_table[:, :],
                            bass.IndirectOffsetOnAxis(ap=fin_rows[:, h, k, WROW:WROW + 1].bitcast(I32), axis=0),
                            fin_rows[:, h, k, 0:WROW], None).then_inc(s_finw[h], 16)
            for h in range(2):
                pool.wait_ge(s_finw[h], 16 * THALF * TITER)
            gather_layer(l1, hA_table, ring1, s_row, 16)

            with pool.Fori(0, TITER) as it:
                for h in range(2):
                    wait_alone(pool, s_outs, 4 * it + 2 * h + 2)
                    for k in range(THALF):
                        pool.indirect_dma_start(
                            out[:, :], bass.IndirectOffsetOnAxis(ap=out_idx[:, h, k, 0:1], axis=0),
                            out_rows[:, h, k, :], None, bounds_check=N - 1,
                            oob_is_err=False).then_inc(s_outw[h], 16)
            for h in range(2):
                pool.wait_ge(s_outw[h], 16 * THALF * TITER)

        @block.sync
        def _(sp):
            with nc.allow_non_contiguous_dma(reason="every ROW-th entry of the sorted list"):
                sp.dma_start(dst_top[:], dst_rows[:, 0:1].rearrange("a b -> (a b)")).then_inc(s_topd, 16)
            sp.wait_ge(s_topd, 16)
            sp.dma_start(top_i[:, :], dst_top[:].unsqueeze(0).to_broadcast([P, TOP])).then_inc(s_top, 16)
            sp.wait_ge(s_zero, 2)
            sp.dma_start(x_nodes[0:FULL], x[0:FULL * T, :].rearrange("(p t) d -> p t d", p=FULL)).then_inc(s_x, 16)
            if REST:
                sp.dma_start(x_nodes[FULL:FULL + 1, 0:REST], x[FULL * T:N, :].unsqueeze(0)).then_inc(s_x, 16)
            flat_src = src_pad.rearrange("a b -> (a b)")
            sp.dma_start(flat_src[0:E], src[:]).then_inc(s_tab, 16)
            sp.dma_start(flat_src[E:E + SRC_PAD].unsqueeze(0), src_tail[0:1, :]).then_inc(s_tab, 16)

            for h in range(2):
                sp.wait_ge(s_recw[h], 16 * THALF * TITER)
            ranks = records.rearrange("(p t) w -> p t w", p=P)
            sp.dma_start(by_rank[:, 0:FIRST, :], ranks[:, 0:FIRST, :]).then_inc(s_rank[0], 16)
            sp.wait_ge(s_rank[0], 16)
            sp.dma_start(by_rank[:, FIRST:T, :], ranks[:, FIRST:T, :]).then_inc(s_rank[1], 16)

            sp.wait_ge(s_ctl, 4)
            sp.sem_inc(s_rfree, 2)

            def write_tiles(it, h):
                _, before = tile_slots(sp, it * (2 * THALF) + h * THALF)
                wait_alone(sp, s_mask, it * (2 * THALF) + (h + 1) * THALF)
                sp.dma_start(stream[:, bass.ds(before, THALF * RUN)], runs_m[:, h, :]).then_inc(s_wr, 16)
                wait_alone(sp, s_wr, it * 32 + 16 * (h + 1))
                sp.sem_inc(s_rfree, 1)

            def load_first_stages():
                for h in range(STAGES):
                    sp.dma_start(stage[:, h, :], stream[:, h * STAGE_COLS:(h + 1) * STAGE_COLS]
                                 ).then_inc(l0.staged[h], 16)

            with sp.Fori(0, TITER - 1) as it:
                for h in range(2):
                    write_tiles(it, h)
            with sp.If(highest_degree(sp) <= RUN):
                load_first_stages()
            for h in range(2):
                write_tiles(TITER - 1, h)
            with sp.If(highest_degree(sp) > RUN):
                with sp.Fori(0, T) as i:
                    n, before = tile_blocks(sp, i)
                    _, slots_before = tile_slots(sp, i)
                    with sp.Fori(0, n) as b:
                        wait_alone(sp, s_blkm, before + b + 1)
                        col = nc.s_assert_within(slots_before + b * RUN, 0, STREAM - RUN,
                                                 skip_runtime_bounds_check_because="a tile's blocks start before its end")
                        sp.dma_start(stream[:, bass.ds(col, RUN)], runs_m[:, 0, 0:RUN]).then_inc(s_blkw, 16)
                        wait_alone(sp, s_blkw, (before + b + 1) * 16)
                load_first_stages()
            slots = sp.value_load(tot[0:1, 0:1], min_val=T, max_val=MAXCOLS)
            sp.dma_start(stream[:, bass.ds(slots, RUN)], zcols[:, :]).then_inc(s_wr, 16)
            sp.wait_ge(s_wr, 16 * (T // THALF + 1))

            def relay_layer(ly, mirror):
                n = groups(sp)
                with sp.Fori(0, n) as g:
                    for h in range(STAGES):
                        for c in range(STAGE_CHUNKS * h, STAGE_CHUNKS * (h + 1)):
                            sp.wait_ge(ly.got[c], 16 * SLOTS * (g + 1))
                            if mirror and c == 0:
                                sp.dma_start(ring1[:, GROUP_COLS:GROUP_COLS + SLOTS - 1, :],
                                             ring1[:, 0:SLOTS - 1, :]).then_inc(s_mirror, 16)
                                sp.wait_ge(s_mirror, 16 * (g + 1))
                            sp.sem_inc(ly.landed, SLOTS)
                        next_cols = bass.ds(g * GROUP_COLS + GROUP_COLS + h * STAGE_COLS, STAGE_COLS)
                        sp.dma_start(stage[:, h, :], stream[:, next_cols]).then_inc(ly.staged[h], 16)
                for h in range(STAGES):
                    wait_alone(sp, ly.staged[h], 16 * (n + 1))

            relay_layer(l0, False)

            half = THALF * (WROW + 1)
            for h in range(2):
                sp.wait_ge(s_row, 16 * (THALF * (h + 1) + 1))
                sp.dma_start(fin_rows[:, h, :, :].rearrange("p t w -> p (t w)"),
                             ranked_rows[:, h * half:(h + 1) * half]).then_inc(s_fin[h], 16)
            with sp.Fori(0, TITER - 1) as it:
                for h in range(2):
                    wait_alone(sp, s_finw[h], 16 * THALF * (it + 1))
                    sp.wait_ge(s_row, it * (32 * THALF) + 16 * (THALF * (h + 3) + 1))
                    sp.dma_start(fin_rows[:, h, :, :].rearrange("p t w -> p (t w)"),
                                 ranked_rows[:, bass.ds(it * (2 * half) + (2 + h) * half, half)]).then_inc(s_fin[h], 16)
            for h in range(STAGES):
                sp.dma_start(stage[:, h, :], stream[:, h * STAGE_COLS:(h + 1) * STAGE_COLS]).then_inc(l1.staged[h], 16)
            relay_layer(l1, True)

        @block.vector
        def _(v):
            st = Steps(v, s_dve, wait_alone)

            def bc(t, n):
                return t.unsqueeze(2).to_broadcast([t.shape[0], t.shape[1], n])

            def bc_mid(t, n):
                return t.unsqueeze(1).to_broadcast([t.shape[0], n, t.shape[1]])

            v.memset(ones[:, :], 1.0).then_inc(s_zero, 1)
            st.done(v.memset(zeros[:, :], 0.0))
            st.done(v.memset(one1[:, :], 1.0))
            st.done(v.memset(src_tail[:, :], 0))
            st.done(v.memset(runs_m[:, :, :], ZROW))
            st.done(v.memset(zcols[:, :], ZROW))
            st.done(v.memset(eps_col[:, :], EPS))
            st.done(v.memset(rec[:, :, :], 0))
            st.link(v.memset(x_nodes[96:P], 0.0))
            v.memset(stats[:, :], 0.0).then_inc(s_zero, 1)

            v.wait_ge(s_const, 6)
            st.link(v.tensor_copy(q[:, :], q_i[:, :]))
            v.tensor_scalar(q_mid[:, :], q[:, :], -0.5, None, ALU.add).then_inc(s_q, 1)
            v.wait_ge(s_top, 16)
            v.tensor_copy(top[:, :], top_i[:, :]).then_inc(s_q, 1)
            st.done(v.tensor_copy(iota_bin[:, :], iota_i[:, 0:BINS]))
            st.done(v.tensor_copy(iota_run[:, :], iota_i[:, :]))
            st.done(v.tensor_copy(tile_rank[:, :], tile_i[:, :]))

            def rows_of(at, after):
                v.wait_ge(s_bal, after)
                st.link(v.tensor_scalar(row[:, at], balance[:, at], 0.5, TOP / 2 - 1, ALU.mult, ALU.add))
                st.link_alone(v.tensor_scalar(row[:, at], row[:, at], 0.0, None, ALU.max))

            def stage_rows(at, a):
                v.tensor_copy(sstage[:, a, :], row[:, at]).then_inc(s_idx, 1)

            def count(it, a):
                v.wait_ge(s_got[a], 16 * PCOLS * (it + 1))
                for k in range(PCOLS):
                    col = bass.ds(it * PASS + a * PCOLS + k, 1)
                    ins = v.tensor_scalar(below_out[:, k, :], got[:, a, k, :], q[:, col], 0.0, ALU.is_lt, ALU.add,
                                          accum_out=below[:, col])
                st.link_alone(ins)

            for a in range(PARTS):
                rows_of(slice(a * PCOLS, (a + 1) * PCOLS), (a + 1) * PCOLS)
                stage_rows(slice(a * PCOLS, (a + 1) * PCOLS), a)
            first, per = st.now(), 2 + PARTS
            with v.Fori(0, SITER - 1) as it:
                st.at(it * per + first)
                rows_of(bass.ds(it * PASS + PASS, PASS), it * PASS + 2 * PASS)
                for a in range(PARTS):
                    count(it, a)
                    stage_rows(bass.ds(it * PASS + PASS + a * PCOLS, PCOLS), a)
                assert st.n == per
            st.at(first + per * (SITER - 1))
            for a in range(PARTS):
                count(SITER - 1, a)
            st.link(v.scalar_tensor_tensor(out=start[:, :], in0=row[:, :], scalar=float(ROW), in1=below[:, :],
                                           op0=ALU.mult, op1=ALU.add))

            st.done(v.tensor_copy(rec[:, :, 0], q_i[:, 0:T]))
            st.done(v.tensor_copy(rec[:, :, 1], start[:, 0:T]))
            st.link(v.tensor_tensor(cols[:, :], start[:, 1:T + 1], start[:, 0:T], ALU.subtract))
            st.done(v.tensor_copy(rec[:, :, 2], cols[:, :]))
            st.link(v.tensor_scalar(bins[:, :], cols[:, :], float(BINS - 1), -1.0, ALU.min, ALU.mult))
            st.link(v.tensor_scalar(bins[:, :], bins[:, :], float(BINS - 1), None, ALU.add))
            st.link(v.tensor_tensor(onehot, bc(iota_bin[:, :], T), bc_mid(bins[:, :], BINS), ALU.is_equal))
            st.link(v.tensor_tensor_scan(order_flat, ones[:, 0:1].to_broadcast([P, BINS * T]), onehot_flat, 0.0,
                                         ALU.mult, ALU.add))
            st.done(v.memset(bin_before[:, 0:1], 0.0))
            st.link(v.tensor_copy(bin_before[:, 1:BINS], order[:, 0:BINS - 1, T - 1]))
            v.tensor_tensor(bin_tot[:, :], order[:, :, T - 1], bin_before[:, :], ALU.subtract).then_inc(s_bins, 1)
            st.link(v.tensor_reduce(top_deg[:, :], cols[:, :], AX.X, ALU.max))
            v.wait_ge(s_binp, 1)
            st.link(v.tensor_copy(bin_tot[:, :], ps_t[:, 0:BINS]))
            st.link(v.tensor_tensor_scan(bin_scan[:, :], ones[:, 0:BINS], bin_tot[:, :], 0.0, ALU.mult, ALU.add))
            v.tensor_scalar(below_out[:, 0, 0:BINS], bin_scan[:, :], tile_rank[:, 0:1], 0.0, ALU.is_lt, ALU.add,
                            accum_out=classes[:, 0:1]).then_inc(s_degf, 1)
            st.link(v.tensor_tensor(bin_scan[:, :], bin_scan[:, :], bin_tot[:, :], ALU.subtract))
            st.link(v.tensor_tensor(bin_off[:, :], bin_scan[:, :], ps_u[:, 0:BINS], ALU.add))
            st.link(v.tensor_tensor(bin_off[:, :], bin_off[:, :], bin_before[:, :], ALU.subtract))

            def rank_nodes(lo, hi):
                at = slice(lo, hi)
                st.link(v.scalar_tensor_tensor(out=order[:, :, at], in0=order[:, :, at], scalar=-1.0,
                                               in1=bc(bin_off[:, :], hi - lo), op0=ALU.add, op1=ALU.add))
                st.link(v.tensor_tensor(order[:, :, at], order[:, :, at], onehot[:, :, at], ALU.mult))
                st.link(v.tensor_reduce(cols2[:, at], order[:, :, at].rearrange("p b t -> p t b"), AX.X, ALU.add))
                st.link(v.tensor_copy(icols[:, at], cols2[:, at]))
                st.done(v.tensor_single_scalar(icols2[:, at], icols[:, at], P - 1, ALU.bitwise_and))
                st.link(v.tensor_single_scalar(icols[:, at], icols[:, at], P.bit_length() - 1, ALU.logical_shift_right))
                st.done(v.tensor_copy(cols2[:, at], icols2[:, at]))
                st.link(v.tensor_copy(cols3[:, at], icols[:, at]))
                st.link(v.scalar_tensor_tensor(out=cols[:, at], in0=cols2[:, at], scalar=float(T), in1=cols3[:, at],
                                               op0=ALU.mult, op1=ALU.add))
                st.link(v.tensor_copy(rec[:, at, 4], cols[:, at]))

            def stage_record(tiles_at, h):
                v.tensor_copy(rank_rec[:, h, :, 0:D], x_nodes[:, tiles_at, :]).then_inc(s_rec, 1)
                v.tensor_copy(rank_rec[:, h, :, D:].bitcast(I32), rec[:, tiles_at, :]).then_inc(s_rec, 1)

            def layer_norm_relu(rows, to, scratch, n, count):
                st.link(v.tensor_reduce(cols[:, 0:n], rows, AX.X, ALU.add))
                st.link(v.tensor_scalar(cols[:, 0:n], cols[:, 0:n], 1.0 / D, None, ALU.mult))
                st.link(v.tensor_tensor(to, rows, bc(cols[:, 0:n], D), ALU.subtract))
                st.link(v.tensor_tensor(scratch, to, to, ALU.mult))
                v.tensor_reduce(cols2[:, 0:n], scratch, AX.X, ALU.add).then_inc(s_var, 1)
                v.wait_ge(s_std, count)
                st.link(v.reciprocal(cols3[:, 0:n], cols3[:, 0:n]))
                st.link(v.tensor_tensor(to, to, bc(cols3[:, 0:n], D), ALU.mult))
                return v.tensor_scalar(to, to, 0.0, None, ALU.max)

            def first_h(tiles_at, count):
                layer_norm_relu(x_nodes[:, tiles_at, :], h_nodes[:, tiles_at, :], hr[:, 0:THALF, :], THALF, count
                                ).then_inc(s_h0, 1)

            rank_nodes(0, 2 * THALF)
            v.wait_ge(s_x, X_DMAS)
            for h in range(2):
                stage_record(slice(h * THALF, (h + 1) * THALF), h)
            rank_nodes(2 * THALF, T)
            first, per = st.now(), 6 * 2
            with v.Fori(0, TITER - 1) as it:
                st.at(it * per + first)
                for h in range(2):
                    first_h(bass.ds(it * (2 * THALF) + h * THALF, THALF), it * 2 + h + 1)
                    wait_alone(v, s_recw[h], 16 * THALF * (it + 1))
                    stage_record(bass.ds(it * (2 * THALF) + (2 + h) * THALF, THALF), h)
                assert st.n == per
            st.at(first + per * (TITER - 1))

            v.wait_ge(s_mxr, 1)
            st.link(v.tensor_reduce(over[:, :], ps_h[0:1, P:2 * P], AX.X, ALU.max))
            st.link(v.tensor_copy(tot[:, 2:3], over[:, :]))
            st.link(v.tensor_scalar(over[:, :], over[:, :], float(1 - BINS), 0.0, ALU.add, ALU.max))
            st.link(v.tensor_scalar(crow[:, 1, :], ps_h[0:1, 0:T], 0.0, None, ALU.is_equal))
            st.link(v.tensor_tensor(crow[:, 1, :], crow[:, 1, :], over[:, :].to_broadcast([1, T]), ALU.mult))
            st.link(v.tensor_scalar(crow[:, 0, :], ps_h[0:1, 0:T], -1.0, float(BINS - 1), ALU.mult, ALU.add))
            st.link(v.tensor_tensor(crow[:, 0, :], crow[:, 0, :], crow[:, 1, :], ALU.add))

            def word_sums(value, at):
                st.link(v.tensor_copy(ctl[:, :, at], value))
                st.link(v.tensor_tensor_scan(crow[:, 3, :], one1[:, :], value, 0.0, ALU.mult, ALU.add))
                if at == 0:
                    st.link(v.tensor_copy(tot[:, 0:1], crow[:, 3, T - 1:T]))
                    st.link(v.tensor_scalar(cols[0:1, 1:2], crow[:, 3, T - 1:T], float(GROUP_COLS - 1), None, ALU.add))
                    st.link(v.tensor_copy(tot[:, 3:4], cols[0:1, 1:2]))
                    st.link(v.tensor_single_scalar(tot[:, 1:2], tot[:, 3:4], GROUP_COLS.bit_length() - 1,
                                                   ALU.logical_shift_right))
                st.link(v.tensor_tensor(crow[:, 3, :], crow[:, 3, :], value, ALU.subtract))
                st.link(v.tensor_copy(ctl[:, :, at + 1], crow[:, 3, :]))

            def rounded_up(value, unit, to, at_least):
                st.link(v.tensor_scalar(crow[:, 3, :], value, float(unit - 1), None, ALU.add))
                st.link(v.tensor_copy(irow[:, 0, :], crow[:, 3, :]))
                st.link(v.tensor_single_scalar(irow[:, 1, :], irow[:, 0, :], unit.bit_length() - 1,
                                               ALU.logical_shift_right))
                st.link(v.tensor_copy(to, irow[:, 1, :]))
                st.link(v.tensor_scalar(to, to, float(at_least), None, ALU.max))

            st.link(v.tensor_scalar(crow[:, 1, :], crow[:, 0, :], float(SLOTS + 1), None, ALU.max))
            word_sums(crow[:, 1, :], 0)
            halves = crow[:, 3, :].rearrange("p (h t) -> p h t", t=THALF)
            st.link(v.tensor_tensor(crow[:, 2, :].rearrange("p (h t) -> p h t", t=THALF), halves,
                                    halves[:, :, 0:1].to_broadcast([1, T // THALF, THALF]), ALU.subtract))
            st.link(v.tensor_tensor(crow[:, 2, :], crow[:, 2, :], merge_max[:, :], ALU.min))
            st.link(v.tensor_copy(ctl[:, :, 4], crow[:, 2, :]))
            rounded_up(crow[:, 0, :], RUN, crow[:, 2, :], 1)
            word_sums(crow[:, 2, :], 2)
            rounded_up(crow[:, 1, :], SLOTS, crow[:, 2, :], 2)
            word_sums(crow[:, 2, :], 5)
            st.link(v.tensor_copy(crow[:, 0, :], ctl[:, :, 1]))
            st.link(v.tensor_tensor(crow[:, 0, :], crow[:, 0, :], crow[:, 1, :], ALU.add))
            st.link(v.tensor_scalar(crow[:, 2, :], crow[:, 2, :], float(-SLOTS), float(SLOTS), ALU.mult, ALU.add))
            st.link(v.tensor_tensor(crow[:, 0, :], crow[:, 0, :], crow[:, 2, :], ALU.add))
            st.link(v.tensor_copy(ctl[:, :, 7], crow[:, 0, :]))
            v.memset(top_deg[:, :], 0.0).then_inc(s_ctl, 4)
            v.wait_ge(s_ctl, 4)

            def stage_tiles(tiles_at, h):
                v.tensor_copy(tstage[:, h, :, :], ranked[:, tiles_at, 0:2]).then_inc(s_tidx, 1)

            v.wait_ge(s_rank[0], 16)
            for h in range(2):
                stage_tiles(slice(h * THALF, (h + 1) * THALF), h)
            st.link(v.tensor_copy(deg[:, 0:FIRST], ranked[:, 0:FIRST, 2]))
            for h in range(2):
                first_h(slice(T - (2 - h) * THALF, T - (1 - h) * THALF), 2 * TITER - 1 + h)

            def mask(got, to, rest, steps, scratch):
                steps.link(v.tensor_tensor(scratch[0], scratch[1], rest, ALU.is_lt))
                steps.link(v.scalar_tensor_tensor(out=scratch[0], in0=got, scalar=float(-ZROW), in1=scratch[0],
                                                  op0=ALU.add, op1=ALU.mult))
                return v.tensor_scalar(to, scratch[0], float(ZROW), None, ALU.add)

            def take_tiles(it, h):
                wait_alone(v, s_land[h], 16 * THALF * (it + 1))
                wait_alone(v, s_rfree, 2 * it + h + 1)
                first_tile = it * (2 * THALF) + h * THALF
                st.link(v.tensor_tensor(valid[:, :, :], bc_mid(iota_run[:, :], THALF),
                                        bc(deg[:, bass.ds(first_tile, THALF)], RUN), ALU.is_lt))
                st.link_alone(v.scalar_tensor_tensor(out=valid[:, :, :], in0=runs[:, h, :, :], scalar=float(-ZROW),
                                                     in1=valid[:, :, :], op0=ALU.add, op1=ALU.mult))
                for k in range(THALF):
                    at = tile_word(v, first_tile + k, 4, 0, (THALF - 1) * RUN)
                    v.tensor_scalar(runs_m[:, h, bass.ds(at, RUN)], valid[:, k, :], float(ZROW), None,
                                    ALU.add).then_inc(s_mask, 1)
                    wait_alone(v, s_mask, first_tile + k + 1)

            for h in range(2):
                take_tiles(0, h)
                stage_tiles(slice((2 + h) * THALF, (3 + h) * THALF), h)
            v.wait_ge(s_rank[1], 16)
            st.link(v.tensor_copy(deg[:, FIRST:T], ranked[:, FIRST:T, 2]))
            st.link(v.tensor_scalar(rdeg[:, :], deg[:, :], 1.0, None, ALU.max))
            st.link(v.reciprocal(rdeg[:, :], rdeg[:, :]))
            first, per = st.now(), 2 * 2
            with v.Fori(1, TITER - 1) as it:
                st.at(it * per + (first - per))
                for h in range(2):
                    take_tiles(it, h)
                    stage_tiles(bass.ds(it * (2 * THALF) + (2 + h) * THALF, THALF), h)
                assert st.n == per
            st.at(first + per * (TITER - 2))
            for h in range(2):
                take_tiles(TITER - 1, h)

            gen = Steps(v, s_gen, wait_alone)
            offset, left = cols2[:, 0:1], cols2[:, 1:2]
            with v.If(highest_degree(v) > RUN):
                wait_alone(v, s_wr, 16 * (T // THALF))
                with v.Fori(0, T) as i:
                    n, before = tile_blocks(v, i)
                    gen.at((before * 4) + (i * 2))
                    gen.done(v.tensor_copy(offset, at_tile(ranked, i, 1, 2)))
                    gen.link_alone(v.tensor_copy(left, at_tile(ranked, i, 2, 3)))
                    with v.Fori(0, n) as b:
                        gen.at((before + b) * 4 + (i * 2 + 2))
                        v.tensor_scalar(tstage[:, 0, 0, 1:2], offset, float(E), None, ALU.min).then_inc(s_blk, 1)
                        v.wait_ge(s_blkl, (before + b + 1) * 16)
                        v.wait_ge(s_blk, before + b + 1)
                        mask(runs[:, 0, 0, :], runs_m[:, 0, 0:RUN], left.to_broadcast([P, RUN]), gen,
                             (valid[:, 0, :], iota_run[:, :])).then_inc(s_blkm, 1)
                        gen.done(v.tensor_scalar(offset, offset, float(RUN), None, ALU.add))
                        gen.link(v.tensor_scalar(left, left, float(-RUN), None, ALU.add))
                        wait_alone(v, s_blkm, before + b + 1)
                        wait_alone(v, s_blkw, (before + b + 1) * 16)
                        v.nop()

            v.wait_ge(s_h0w, H0_DMAS)
            st.link_alone(layer_norm_relu(xr, hr[:, :, :], x_nodes, T, 2 * TITER + 1))

            first, per = st.now(), 6
            with v.Fori(0, T) as i:
                st.at(i * per + first)
                v.wait_ge(l0.sum, i + 1)
                v.tensor_scalar(cat[:, D:2 * D], ps_sum[:, 0:D], rdeg[:, bass.ds(i, 1)], None,
                                ALU.mult).then_inc(l0.cat, 1)
                v.tensor_copy(cat[:, 0:D], at_tile(hr, i)).then_inc(l0.cat, 1)
                v.wait_ge(l0.y, i + 1)
                st.link_alone(v.scalar_tensor_tensor(out=at_tile(xr, i), in0=ps_y[:, 0:D], scalar=0.0,
                                                     in1=at_tile(xr, i), op0=ALU.max, op1=ALU.add))
                st.link_alone(v.bn_stats(stats[:, :], at_tile(xr, i)))
                v.bn_aggr(mv[:, :], stats[:, :]).then_inc(s_var1, 1)
                v.wait_ge(s_std1, i + 1)
                st.link(v.reciprocal(rstd[:, :], std[:, :]))
                v.wait_ge(s_row, 16 * (i + 1))
                st.link(v.tensor_scalar(rowbuf[:, 0:D], at_tile(xr, i), mv[:, 0:1], rstd[:, 0:1],
                                        ALU.subtract, ALU.mult))
                v.tensor_scalar(rowbuf[:, 0:D], rowbuf[:, 0:D], 0.0, None, ALU.max).then_inc(s_h1, 1)
                wait_alone(v, s_h1, i + 1)
                st.done(v.tensor_copy(at_tile(hr, i), rowbuf[:, 0:D]))
                st.link_alone(v.tensor_copy(rowbuf[:, WROW:WROW + 1].bitcast(I32), at_tile(ranked, i, 0, 1)))
                wait_alone(v, s_ab, i + 1)
                v.tensor_copy(at_tile(b_self, i), ps_h[:, 0:H]).then_inc(l0.tile, 1)
                assert st.n == per
            st.at(first + per * T)

            v.wait_ge(l0.tile, T)
            v.wait_ge(s_ctl, 4)
            first = st.now()

            def rows_at(slot):
                return ring1[:, bass.ds(slot & (GROUP_COLS - 1), SLOTS), :]

            def pre_act(slot, i):
                v.wait_ge(l1.landed, slot + SLOTS)
                v.tensor_tensor(pre[:, :, :], rows_at(slot)[:, :, D:WROW],
                                b_self[:, bass.ds(i, 1), :].to_broadcast([P, SLOTS, H]), ALU.add).then_inc(s_pre, 1)

            def weigh(w):
                v.wait_ge(s_pre, w + 1)
                v.scalar_tensor_tensor(out=act_w[:, :, :], in0=pre[:, :, :], scalar=0.0,
                                       in1=bc_mid(we2_rows[:, :], SLOTS), op0=ALU.max, op1=ALU.mult).then_inc(s_act, 1)

            def score(w):
                v.wait_ge(s_act, w + 1)
                v.tensor_reduce(z[:, :], act_w[:, :, :], AX.X, ALU.add).then_inc(s_z, 1)

            def message(w, slot):
                v.wait_ge(s_gate, w + 1)
                v.wait_ge(s_msgf, w + 1)
                v.tensor_tensor(msg[:, :, :], rows_at(slot)[:, :, 0:D], bc(gate[:, :], D),
                                ALU.mult).then_inc(s_msg, 1)

            def chunk_maximum(w):
                v.wait_ge(s_msg, w + 1)
                v.wait_ge(s_acc, w + 1)
                v.tensor_reduce(chunk_max[:, :], msg[:, :, :].rearrange("p s d -> p d s"), AX.X,
                                ALU.max).then_inc(s_cmax, 1)

            def maximum(w):
                v.wait_ge(s_cmax, w + 1)
                v.tensor_tensor(cat[:, 0:D], cat[:, 0:D], chunk_max[:, :], ALU.max).then_inc(s_acc, 1)

            def finish(i):
                v.wait_ge(l1.y, i + 1)
                st.link(v.tensor_tensor(rowbuf[:, 0:D], ps_y[:, 0:D], at_tile(hr, i), ALU.add))
                st.done(v.tensor_tensor(at_tile(xr, i), rowbuf[:, 0:D], at_tile(xr, i), ALU.add))

            def tile(i, before_it):
                slots, slots_before = tile_slots(v, i)
                n, before = tile_chunks(v, i)
                slot_1 = tile_word(v, i, 7, 1, MAXCOLS)
                if before_it is not None:
                    wait_alone(v, l1.catT, i)
                st.link_alone(v.memset(cat[:, 0:D], 0.0))

                def beside(w, slot, slot_before):
                    pre_act(slot, i)
                    message(w - 1, slot_before)
                    weigh(w)
                    chunk_maximum(w - 1)
                    score(w)
                    maximum(w - 1)

                pre_act(slots_before, i)
                weigh(before)
                score(before)
                if before_it is not None:
                    finish(before_it)
                w = v.snap(before + 1)
                beside(w, slot_1, slots_before)
                with v.If(n > 2):
                    with v.Fori(1, n - 1) as c:
                        w = v.snap(before + c + 1)
                        slot = v.snap(slot_1 + c * SLOTS)
                        beside(w, slot, slot - SLOTS)
                last = v.snap(before + n - 1)
                message(last, slots_before + slots - SLOTS)
                chunk_maximum(last)
                maximum(last)
                wait_alone(v, l1.sum, i + 1)
                v.tensor_copy(h_tile[:, :], at_tile(hr, i)).then_inc(l1.cat, 1)
                v.tensor_copy(cat[:, D:2 * D], ps_sum[:, 0:D]).then_inc(l1.cat, 1)

            v.sem_inc(s_acc, 1)
            tile(0, None)
            first, per = st.now(), 3
            with v.Fori(1, T - 1) as i:
                st.at(i * per + (first - per))
                tile(i, i - 1)
                assert st.n == per
            st.at(first + per * (T - 2))

            def stage_out(tiles_at, h):
                v.tensor_copy(out_rows[:, h, :, :], xr[:, tiles_at, :]).then_inc(s_outs, 1)
                v.tensor_copy(out_idx[:, h, :, :], ranked[:, tiles_at, 0:2]).then_inc(s_outs, 1)

            wait_alone(v, s_dve, st.now())
            for h in range(2):
                stage_out(slice(h * THALF, (h + 1) * THALF), h)
            tile(T - 1, T - 2)
            finish(T - 1)
            st.wait()
            with v.Fori(0, TITER - 1) as it:
                for h in range(2):
                    wait_alone(v, s_outw[h], 16 * THALF * (it + 1))
                    stage_out(bass.ds(it * (2 * THALF) + (2 + h) * THALF, THALF), h)

        @block.scalar
        def _(act):
            def load(to, frm):
                act.dma_start(to, frm).then_inc(s_w, 16)

            act.wait_ge(s_q, 2)
            with act.Fori(0, SITER) as it:
                for k in range(PASS):
                    col = bass.ds(it * PASS + k, 1)
                    act.activation(signs[:, k, :], top[:, :], ACT.Sign, scale=-1.0, bias=q_mid[:, col],
                                   accum_out=balance[:, col]).then_inc(s_bal, 1)
                wait_alone(act, s_bal, it * PASS + PASS)

            load(w_cat[0:D, :], w_self[:, :])
            load(w_cat[D:2 * D, :], w_neigh[:, :])
            load(w_ab[:, 0:H], we1[0:D, :])
            load(w_ab[:, H:2 * H], we1[D:2 * D, :])
            load(w_n1a[:, :], wn1[0:2 * D, :])
            load(w_n1b[:, :], wn1[2 * D:3 * D, :])
            load(w_n2[:, :], wn2[:, :])
            load(b0_row[:, :], b0[:].unsqueeze(0))
            load(bn2_row[:, :], bn2[:].unsqueeze(0))
            load(bn1_col[:, :], bn1[:].unsqueeze(1))
            load(be2_col[:, :], be2[:].unsqueeze(0).to_broadcast([P, 1]))
            load(we2_rows[:, :], we2.rearrange("h a -> a h").to_broadcast([P, H]))
            load(be1_row[:, :], be1[:].unsqueeze(0))
            act.dma_start(h0_table[ZROW:ZROW + 1, :], zeros[0:1, 0:D]).then_inc(s_h0w, 16)
            act.dma_start(hA_table[ZROW:ZROW + 1, :], zeros[0:1, :]).then_inc(s_row, 16)

            h0_by_node = h0_table[0:NP, :].rearrange("(p t) d -> p (t d)", p=P)
            with act.Fori(0, 2 * TITER) as g:
                act.wait_ge(s_var, g + 1)
                act.activation(cols3[:, 0:THALF], cols2[:, 0:THALF], ACT.Sqrt, bias=eps_col[:, 0:1],
                               scale=1.0 / D).then_inc(s_std, 1)
                wait_alone(act, s_h0, g + 1)
                act.dma_start(h0_by_node[:, bass.ds(g * (THALF * D), THALF * D)],
                              h_nodes[:, bass.ds(g * THALF, THALF), :]).then_inc(s_h0w, 16)
            act.wait_ge(s_var, 2 * TITER + 1)
            act.activation(cols3[:, :], cols2[:, :], ACT.Sqrt, bias=eps_col[:, 0:1], scale=1.0 / D).then_inc(s_std, 1)

            act.wait_ge(s_w, W_DMAS)
            with act.Fori(0, T) as i:
                act.wait_ge(l0.catT, i + 1)
                act.activation(catT[:, :], ps_t[:, 0:P], ACT.Copy).then_inc(l0.catTs, 1)
                act.wait_ge(s_var1, i + 1)
                act.activation(std[:, :], mv[:, 1:2], ACT.Sqrt, bias=eps_col[:, 0:1]).then_inc(s_std1, 1)
                act.wait_ge(s_h1T, i + 1)
                act.activation(hT[:, :], ps_u[0:D, 0:P], ACT.Copy).then_inc(s_h1Ts, 1)
                act.wait_ge(s_ab, i + 1)
                act.activation(rowbuf[:, D:WROW], ps_a[:, 0:H], ACT.Copy).then_inc(s_rowA, 1)
                act.wait_ge(s_rowA, i + 1)
                act.wait_ge(l0.tile, i + 1)
                act.dma_start(ranked_rows[:, bass.ds(i * (WROW + 1), WROW + 1)], rowbuf[:, :]).then_inc(s_row, 16)

            with act.Fori(0, T) as i:
                n, before = tile_chunks(act, i)
                with act.Fori(0, n) as c:
                    w = act.snap(before + c)
                    act.wait_ge(s_z, w + 1)
                    act.activation(gate[:, :], z[:, :], ACT.Sigmoid, bias=be2_col[:, 0:1]).then_inc(s_gate, 1)
                act.wait_ge(l1.catT, i + 1)
                act.activation(catT[:, :], ps_t[:, 0:P], ACT.Copy).then_inc(l1.catTs, 1)
                act.activation(hT[:, :], ps_u[0:D, 0:P], ACT.Copy).then_inc(l1.catTs, 1)
                act.wait_ge(s_hid, i + 1)
                act.activation(h2T[:, :], ps_h[:, 0:P], ACT.Relu, bias=bn1_col[:, 0:1]).then_inc(s_hids, 1)

        @block.tensor
        def _(pe):
            pe.wait_ge(s_const, 6)
            pe.wait_ge(s_bins, 1)
            pe.matmul(ps_t[:, 0:BINS], ones[:, :], bin_tot[:, :], start=True, stop=True)
            pe.matmul(ps_u[:, 0:BINS], upper[:, :], bin_tot[:, :], start=True, stop=True).then_inc(s_binp, 1)
            pe.wait_ge(s_degf, 1)
            pe.transpose(ps_h[0:1, 0:P], classes[:, 0:1], ident[:, :])
            pe.transpose(ps_h[0:1, P:2 * P], top_deg[:, 0:1], ident[:, :]).then_inc(s_mxr, 1)
            pe.wait_ge(s_ctl, 4)
            pe.wait_ge(s_w, W_DMAS)

            def sum_start():
                pe.matmul(ps_sum[:, 0:D], zeros[0:1, 0:P], zeros[0:1, 0:D], start=True, stop=False,
                          skip_group_check=True)

            def sum_add(rows):
                return pe.matmul(ps_sum[:, 0:D], ident[:, :], rows, start=False, stop=False, skip_group_check=True)

            def sum_stop():
                return pe.matmul(ps_sum[:, 0:D], zeros[0:1, 0:P], zeros[0:1, 0:D], start=False, stop=True,
                                 skip_group_check=True)

            pe.sem_inc(l0.used, GROUP_COLS)
            with pe.Fori(0, T) as i:
                slots, slots_before = tile_slots(pe, i)
                sum_start()
                with pe.Fori(slots_before, slots_before + slots) as slot:
                    pe.wait_ge(l0.landed, slot + 1)
                    sum_add(ring0[:, bass.ds(slot & (GROUP_COLS - 1), 1), :].rearrange("p c w -> p (c w)")
                            ).then_inc(l0.used, 1)
                sum_stop().then_inc(l0.sum, 1)
                pe.wait_ge(l0.cat, 2 * i + 2)
                pe.transpose(ps_t[:, 0:P], cat[:, :], ident[:, :]).then_inc(l0.catT, 1)
                pe.wait_ge(l0.catTs, i + 1)
                pe.matmul(ps_y[:, 0:D], catT[:, :], w_cat[:, :], start=True, stop=False)
                pe.matmul(ps_y[:, 0:D], ones[0:1, 0:P], b0_row[:, :], start=False, stop=True).then_inc(l0.y, 1)
                wait_alone(pe, s_h1, i + 1)
                pe.transpose(ps_u[0:D, 0:P], rowbuf[:, 0:D], ident[:, :]).then_inc(s_h1T, 1)
                pe.wait_ge(s_h1Ts, i + 1)
                pe.matmul(ps_a[:, 0:H], hT[:, :], w_ab[:, 0:H], start=True, stop=True)
                pe.matmul(ps_h[:, 0:H], hT[:, :], w_ab[:, H:2 * H], start=True, stop=False)
                pe.matmul(ps_h[:, 0:H], ones[0:1, 0:P], be1_row[:, :], start=False, stop=True).then_inc(s_ab, 1)

            pe.sem_inc(l1.used, GROUP_COLS)
            pe.sem_inc(s_msgf, 1)
            with pe.Fori(0, T) as i:
                slots, _ = tile_slots(pe, i)
                n, before = tile_chunks(pe, i)
                sum_start()
                wait_alone(pe, s_msg, before + 1)
                own = nc.s_assert_within(slots - (n - 1) * SLOTS, 1, SLOTS,
                                         skip_runtime_bounds_check_because="the other chunks are full ones")
                with pe.Fori(0, own) as s:
                    s = nc.s_assert_within(s, 0, SLOTS - 1, skip_runtime_bounds_check_because="a slot of the chunk")
                    sum_add(msg[:, bass.ds(s, 1), :].rearrange("p c w -> p (c w)")).then_inc(l1.used, 1)
                pe.matmul(ps_sum[:, 0:D], zeros[0:1, 0:P], zeros[0:1, 0:D], start=False, stop=False,
                          skip_group_check=True).then_inc(s_msgf, 1)
                with pe.Fori(1, n) as c:
                    w = pe.snap(before + c)
                    pe.wait_ge(s_msg, w + 1)
                    for s in range(SLOTS):
                        last = sum_add(msg[:, s, :])
                    last.then_inc(s_msgf, 1)
                    pe.sem_inc(l1.used, SLOTS)
                sum_stop().then_inc(l1.sum, 1)
                wait_alone(pe, l1.cat, 2 * i + 2)
                pe.transpose(ps_u[0:D, 0:P], h_tile[:, :], ident[:, :])
                pe.transpose(ps_t[:, 0:P], cat[:, :], ident[:, :]).then_inc(l1.catT, 1)
                pe.wait_ge(l1.catTs, 2 * i + 2)
                pe.matmul(ps_h[:, 0:P], w_n1a[:, :], catT[:, :], start=True, stop=False)
                pe.matmul(ps_h[:, 0:P], w_n1b[:, :], hT[:, :], start=False, stop=True).then_inc(s_hid, 1)
                pe.wait_ge(s_hids, i + 1)
                pe.matmul(ps_y[:, 0:D], h2T[:, :], w_n2[:, :], start=True, stop=False)
                pe.matmul(ps_y[:, 0:D], ones[0:1, 0:P], bn2_row[:, :], start=False, stop=True).then_inc(l1.y, 1)


_INS = ['x', 'src', 'dst', 'L0_gnn_W_self', 'L0_gnn_W_neigh', 'L0_gnn_b', 'L1_gnn_We1', 'L1_gnn_be1', 'L1_gnn_We2',
        'L1_gnn_be2', 'L1_gnn_Wn1', 'L1_gnn_bn1', 'L1_gnn_Wn2', 'L1_gnn_bn2']


def kernel(**inputs):
    import numpy as _np
    import concourse.bacc as _bacc
    from concourse import mybir as _mybir
    from concourse.bass_utils import run_bass_kernel_spmd as _run

    nc = _bacc.Bacc("TRN2", target_bir_lowering=False, num_devices=1)
    arrays, args = {}, []
    for name in _INS:
        a = _np.ascontiguousarray(inputs[name])
        arrays[f"in_{name}_dram"] = a
        args.append(nc.dram_tensor(f"in_{name}_dram", a.shape, _mybir.dt.from_np(a.dtype), kind="ExternalInput").ap())
    args.append(nc.dram_tensor("out_dram", inputs['x'].shape, _mybir.dt.float32, kind="ExternalOutput").ap())
    gnn_kernel(nc, *args)
    r = _run(nc, [arrays], core_ids=[0])
    return r.results[0]["out_dram"]
```
